# Optimizing a Trainium2 kernel written in Bass

```python
import numpy as np
import jax
import jax.numpy as jnp

def _softmax(x, axis=-1):
    return jax.nn.softmax(x, axis=axis)

def _gelu(x):
    return jax.nn.gelu(x, approximate=True)

def _silu(x):
    return jax.nn.silu(x)

def _sigmoid(x):
    return jax.nn.sigmoid(x)

def _layernorm(x, axis=-1, eps=1e-05):
    m = jnp.mean(x, axis=axis, keepdims=True)
    v = jnp.var(x, axis=axis, keepdims=True)
    return (x - m) / jnp.sqrt(v + eps)

def _scatter_add(tgt, idx, src, axis=0):
    return tgt.at[idx].add(src)

def _segment_sum(src, seg, n):
    return jax.ops.segment_sum(src, seg, n)
kernel_name = 'mk_cond_seq_d2_seqx_r4_9a159a'

def setup_inputs(seed: int=0):
    np.random.seed(seed)
    _w = jnp.asarray

    def _rec_inputs():
        import jax
        import jax.numpy as jnp
        _rk = jax.random.key(seed)
        x = -0.0002928 + 1 * jax.random.normal(jax.random.fold_in(_rk, 1), (64, 64, 256), jnp.float32)
        _lenS = 64 - jax.random.randint(jax.random.fold_in(_rk, 7), (64,), 0, max(1, 64 // 4) + 1, jnp.int32)
        _lenS2 = 64 - jax.random.randint(jax.random.fold_in(_rk, 8), (64,), 0, max(1, 64 // 4) + 1, jnp.int32)
        cond_1024 = 0.0061147 + 1.02565 * jax.random.normal(jax.random.fold_in(_rk, 11), (64, 256), jnp.float32)
        _validS = jnp.arange(64)[None, :] < _lenS[:, None]
        _validS2 = jnp.arange(64)[None, :] < _lenS2[:, None]
        _causal = jnp.tril(jnp.ones((64, 64), dtype=bool))
        mask_BxS_bf0 = jnp.logical_not(jnp.ones((64, 64), dtype=bool))
        return (x, cond_1024, mask_BxS_bf0)
    x, cond_1024, mask_BxS_bf0 = _rec_inputs()

    def _L0_cond_setup():
        import jax, jax.numpy as jnp
        import numpy as np
        D = 256
        H = 16
        HD = 4 * D
        B, T = (4, 256)
        EPS = 1e-05

        def _layernorm(x, g, b):
            mu = jnp.mean(x, axis=-1, keepdims=True)
            var = jnp.mean(jnp.square(x - mu), axis=-1, keepdims=True)
            return (x - mu) * jax.lax.rsqrt(var + EPS) * g + b

        def _attention(x, Wqkv, Wproj, bproj):
            b, t, c = x.shape
            hd = c // H
            qkv = (x @ Wqkv).reshape(b, t, 3, H, hd).transpose(2, 0, 3, 1, 4)
            q, k, v = (qkv[0], qkv[1], qkv[2])
            scale = hd ** (-0.5)
            scores = jnp.einsum('bhqd,bhkd->bhqk', q, k) * scale
            causal = jnp.tril(jnp.ones((t, t), bool))
            scores = jnp.where(causal, scores, -jnp.inf)
            attn = jax.nn.softmax(scores, axis=-1)
            out = jnp.einsum('bhqk,bhkd->bhqd', attn, v)
            out = out.transpose(0, 2, 1, 3).reshape(b, t, c)
            return out @ Wproj + bproj
        key = jax.random.key(seed)
        ks = jax.random.split(key, 12)
        s = 0.02
        return {'x': jax.random.normal(ks[0], (B, T, D), jnp.float32), 'condition': jax.random.normal(ks[1], (B, D), jnp.float32), 'Wqkv': jax.random.normal(ks[2], (D, 3 * D), jnp.float32) * s, 'Wproj': jax.random.normal(ks[3], (D, D), jnp.float32) * s, 'bproj': jnp.zeros((D,), jnp.float32), 'W1': jax.random.normal(ks[4], (D, HD), jnp.float32) * s, 'b1': jnp.zeros((HD,), jnp.float32), 'W2': jax.random.normal(ks[5], (HD, D), jnp.float32) * s, 'b2': jnp.zeros((D,), jnp.float32), 'g1': jnp.ones((D,), jnp.float32), 'be1': jnp.zeros((D,), jnp.float32), 'g2': jnp.ones((D,), jnp.float32), 'be2': jnp.zeros((D,), jnp.float32), 'Wada': jax.random.normal(ks[6], (D, 6 * D), jnp.float32) * s, 'bada': jax.random.normal(ks[7], (6 * D,), jnp.float32) * s}
    _L0_cond_all = _L0_cond_setup()
    _L0_cond_in = {k: v for k, v in _L0_cond_all.items() if k in ('Wqkv', 'Wproj', 'bproj', 'W1', 'b1', 'W2', 'b2', 'g1', 'be1', 'g2', 'be2', 'Wada', 'bada')}
    del _L0_cond_all

    def _L1_cond_setup():
        import math
        import jax, jax.numpy as jnp
        import numpy as np
        H = 256
        NH = 16
        HD = H // NH
        CD = 256
        MLP = 1024
        EPS = 1e-05

        def _layernorm(x):
            mu = jnp.mean(x, axis=-1, keepdims=True)
            var = jnp.var(x, axis=-1, keepdims=True)
            return (x - mu) * jax.lax.rsqrt(var + EPS)

        def _adaln(x, cond, W, b):
            ss = cond @ W.T + b
            scale, shift = jnp.split(ss, 2, axis=-1)
            return _layernorm(x) * (1.0 + scale[:, None, :]) + shift[:, None, :]
        key = jax.random.key(seed)
        ks = jax.random.split(key, 16)
        s = 0.02
        inp = {'x': jax.random.normal(ks[0], (2, 512, H), jnp.float32), 'cond': jax.random.normal(ks[1], (2, CD), jnp.float32), 'key_padding_mask': jnp.zeros((2, 512), dtype=bool), 'w_adaln1': jax.random.normal(ks[2], (2 * H, CD), jnp.float32) * s, 'b_adaln1': jnp.zeros((2 * H,), jnp.float32), 'w_adaln2': jax.random.normal(ks[3], (2 * H, CD), jnp.float32) * s, 'b_adaln2': jnp.zeros((2 * H,), jnp.float32), 'wq': jax.random.normal(ks[4], (H, H), jnp.float32) * s, 'bq': jnp.zeros((H,), jnp.float32), 'wk': jax.random.normal(ks[5], (H, H), jnp.float32) * s, 'bk': jnp.zeros((H,), jnp.float32), 'wv': jax.random.normal(ks[6], (H, H), jnp.float32) * s, 'bv': jnp.zeros((H,), jnp.float32), 'wo': jax.random.normal(ks[7], (H, H), jnp.float32) * s, 'bo': jnp.zeros((H,), jnp.float32), 'w1': jax.random.normal(ks[8], (MLP, H), jnp.float32) * s, 'b1': jnp.zeros((MLP,), jnp.float32), 'w2': jax.random.normal(ks[9], (H, MLP), jnp.float32) * s, 'b2': jnp.zeros((H,), jnp.float32)}
        return inp
    _L1_cond_all = _L1_cond_setup()
    _L1_cond_in = {k: v for k, v in _L1_cond_all.items() if k in ('w_adaln1', 'b_adaln1', 'w_adaln2', 'b_adaln2', 'wq', 'bq', 'wk', 'bk', 'wv', 'bv', 'wo', 'bo', 'w1', 'b1', 'w2', 'b2')}
    del _L1_cond_all
    return {'x': x, 'cond_1024': cond_1024, 'mask_BxS_bf0': mask_BxS_bf0, 'L0_cond_Wqkv': _L0_cond_in['Wqkv'], 'L0_cond_Wproj': _L0_cond_in['Wproj'], 'L0_cond_bproj': _L0_cond_in['bproj'], 'L0_cond_W1': _L0_cond_in['W1'], 'L0_cond_b1': _L0_cond_in['b1'], 'L0_cond_W2': _L0_cond_in['W2'], 'L0_cond_b2': _L0_cond_in['b2'], 'L0_cond_g1': _L0_cond_in['g1'], 'L0_cond_be1': _L0_cond_in['be1'], 'L0_cond_g2': _L0_cond_in['g2'], 'L0_cond_be2': _L0_cond_in['be2'], 'L0_cond_Wada': _L0_cond_in['Wada'], 'L0_cond_bada': _L0_cond_in['bada'], 'L1_cond_w_adaln1': _L1_cond_in['w_adaln1'], 'L1_cond_b_adaln1': _L1_cond_in['b_adaln1'], 'L1_cond_w_adaln2': _L1_cond_in['w_adaln2'], 'L1_cond_b_adaln2': _L1_cond_in['b_adaln2'], 'L1_cond_wq': _L1_cond_in['wq'], 'L1_cond_bq': _L1_cond_in['bq'], 'L1_cond_wk': _L1_cond_in['wk'], 'L1_cond_bk': _L1_cond_in['bk'], 'L1_cond_wv': _L1_cond_in['wv'], 'L1_cond_bv': _L1_cond_in['bv'], 'L1_cond_wo': _L1_cond_in['wo'], 'L1_cond_bo': _L1_cond_in['bo'], 'L1_cond_w1': _L1_cond_in['w1'], 'L1_cond_b1': _L1_cond_in['b1'], 'L1_cond_w2': _L1_cond_in['w2'], 'L1_cond_b2': _L1_cond_in['b2']}

def reference(x, cond_1024, mask_BxS_bf0, L0_cond_Wqkv, L0_cond_Wproj, L0_cond_bproj, L0_cond_W1, L0_cond_b1, L0_cond_W2, L0_cond_b2, L0_cond_g1, L0_cond_be1, L0_cond_g2, L0_cond_be2, L0_cond_Wada, L0_cond_bada, L1_cond_w_adaln1, L1_cond_b_adaln1, L1_cond_w_adaln2, L1_cond_b_adaln2, L1_cond_wq, L1_cond_bq, L1_cond_wk, L1_cond_bk, L1_cond_wv, L1_cond_bv, L1_cond_wo, L1_cond_bo, L1_cond_w1, L1_cond_b1, L1_cond_w2, L1_cond_b2):
    import jax
    import jax.numpy as jnp

    def _L0_cond_ref(x, condition, Wqkv, Wproj, bproj, W1, b1, W2, b2, g1, be1, g2, be2, Wada, bada):
        import jax, jax.numpy as jnp
        import numpy as np
        D = 256
        H = 16
        HD = 4 * D
        B, T = (4, 256)
        EPS = 1e-05

        def _layernorm(x, g, b):
            mu = jnp.mean(x, axis=-1, keepdims=True)
            var = jnp.mean(jnp.square(x - mu), axis=-1, keepdims=True)
            return (x - mu) * jax.lax.rsqrt(var + EPS) * g + b

        def _attention(x, Wqkv, Wproj, bproj):
            b, t, c = x.shape
            hd = c // H
            qkv = (x @ Wqkv).reshape(b, t, 3, H, hd).transpose(2, 0, 3, 1, 4)
            q, k, v = (qkv[0], qkv[1], qkv[2])
            scale = hd ** (-0.5)
            scores = jnp.einsum('bhqd,bhkd->bhqk', q, k) * scale
            causal = jnp.tril(jnp.ones((t, t), bool))
            scores = jnp.where(causal, scores, -jnp.inf)
            attn = jax.nn.softmax(scores, axis=-1)
            out = jnp.einsum('bhqk,bhkd->bhqd', attn, v)
            out = out.transpose(0, 2, 1, 3).reshape(b, t, c)
            return out @ Wproj + bproj
        mod = jax.nn.silu(condition) @ Wada + bada
        sh_a, sc_a, gt_a, sh_m, sc_m, gt_m = jnp.split(mod, 6, axis=1)
        xn = _layernorm(x, g1, be1)
        xm = xn * (1.0 + sc_a[:, None, :]) + sh_a[:, None, :]
        x = x + gt_a[:, None, :] * _attention(xm, Wqkv, Wproj, bproj)
        xn = _layernorm(x, g2, be2)
        xm = xn * (1.0 + sc_m[:, None, :]) + sh_m[:, None, :]
        h = jax.nn.gelu(xm @ W1 + b1, approximate=False)
        x = x + gt_m[:, None, :] * (h @ W2 + b2)
        return x

    def _L1_cond_ref(x, cond, key_padding_mask, w_adaln1, b_adaln1, w_adaln2, b_adaln2, wq, bq, wk, bk, wv, bv, wo, bo, w1, b1, w2, b2):
        import math
        import jax, jax.numpy as jnp
        import numpy as np
        H = 256
        NH = 16
        HD = H // NH
        CD = 256
        MLP = 1024
        EPS = 1e-05

        def _layernorm(x):
            mu = jnp.mean(x, axis=-1, keepdims=True)
            var = jnp.var(x, axis=-1, keepdims=True)
            return (x - mu) * jax.lax.rsqrt(var + EPS)

        def _adaln(x, cond, W, b):
            ss = cond @ W.T + b
            scale, shift = jnp.split(ss, 2, axis=-1)
            return _layernorm(x) * (1.0 + scale[:, None, :]) + shift[:, None, :]
        B, L, D = x.shape
        normed = _adaln(x, cond, w_adaln1, b_adaln1)
        q = (normed @ wq.T + bq).reshape(B, L, NH, HD)
        k = (normed @ wk.T + bk).reshape(B, L, NH, HD)
        v = (normed @ wv.T + bv).reshape(B, L, NH, HD)
        scale = math.sqrt(HD)
        scores = jnp.einsum('blhd,bmhd->bhlm', q, k) / scale
        scores = jnp.where(key_padding_mask[:, None, None, :], -jnp.inf, scores)
        attn = jax.nn.softmax(scores, axis=-1)
        attn_out = jnp.einsum('bhlm,bmhd->blhd', attn, v).reshape(B, L, D)
        x = x + attn_out @ wo.T + bo
        normed = _adaln(x, cond, w_adaln2, b_adaln2)
        h = jax.nn.gelu(normed @ w1.T + b1, approximate=False)
        x = x + h @ w2.T + b2
        return x
    x = _L0_cond_ref(x, cond_1024, L0_cond_Wqkv, L0_cond_Wproj, L0_cond_bproj, L0_cond_W1, L0_cond_b1, L0_cond_W2, L0_cond_b2, L0_cond_g1, L0_cond_be1, L0_cond_g2, L0_cond_be2, L0_cond_Wada, L0_cond_bada)
    x = _L1_cond_ref(x, cond_1024, mask_BxS_bf0, L1_cond_w_adaln1, L1_cond_b_adaln1, L1_cond_w_adaln2, L1_cond_b_adaln2, L1_cond_wq, L1_cond_bq, L1_cond_wk, L1_cond_bk, L1_cond_wv, L1_cond_bv, L1_cond_wo, L1_cond_bo, L1_cond_w1, L1_cond_b1, L1_cond_w2, L1_cond_b2)
    return x

_drawn_inputs = setup_inputs


def setup_inputs(seed=0):
    import zlib

    import numpy as np

    out = dict(_drawn_inputs(seed))
    spreads = {'L0_cond_bproj': (0.0, 0.399),
     'L0_cond_b1': (0.0, 0.8),
     'L0_cond_b2': (0.0, 0.444),
     'L0_cond_g1': (1.0, 0.6),
     'L0_cond_be1': (0.0, 0.8),
     'L0_cond_g2': (1.0, 0.6),
     'L0_cond_be2': (0.0, 2.0),
     'L1_cond_b_adaln1': (0.0, 0.8),
     'L1_cond_b_adaln2': (0.0, 0.51),
     'L1_cond_bq': (0.0, 2.0),
     'L1_cond_bk': (0.0, 2.0),
     'L1_cond_bv': (0.0, 0.272),
     'L1_cond_bo': (0.0, 0.1),
     'L1_cond_b1': (0.0, 0.552),
     'L1_cond_b2': (0.0, 0.1)}
    factors = {'L0_cond_Wqkv': 7.677,
     'L0_cond_Wproj': 7.602,
     'L0_cond_bada': 8.0,
     'L1_cond_wq': 8.0,
     'L1_cond_wk': 8.0,
     'L0_cond_W1': 2.677,
     'L1_cond_w_adaln2': 2.702}
    for name, (base, spread) in spreads.items():
        noise = np.random.default_rng([zlib.crc32(name.encode()), seed]).standard_normal(out[name].shape)
        drawn = base * np.exp(spread * noise) if base else spread * noise
        out[name] = jnp.asarray(drawn.astype(out[name].dtype))
    for name, factor in factors.items():
        out[name] = (out[name] * factor).astype(out[name].dtype)
    return out
```

```python
from contextlib import ExitStack

import numpy as np

import concourse.bass as bass
from concourse import mybir

F32 = mybir.dt.float32
BF16 = mybir.dt.bfloat16
U8 = mybir.dt.uint8
ALU = mybir.AluOpType
ACT = mybir.ActivationFunctionType
AX = mybir.AxisListType

P = 128
NSEQ, S, D = 64, 64, 256
H, HD = 16, 16
MLP = 1024
BS = 8
NB = NSEQ // BS
BT = BS * S
NT = BT // P
KT = D // P
MC = MLP // P
PAIRS = P // (2 * HD)
PP = H // 4
VW = 4 * HD + 2
OT0 = 384
EPS = 1e-5
MASKED = -1e30
SCALE = HD ** -0.5
GROUP = 2

COLS = {}
for _name, _n in (("g1", 2), ("be1", 2), ("g2", 2), ("be2", 2), ("bada_sc_a", 2), ("bada_sh_a", 2),
                  ("bada_sc_m", 2), ("bada_sh_m", 2), ("b1_0", 8), ("sc1_1", 2), ("sh1_1", 2),
                  ("sc2_1", 2), ("sh2_1", 2), ("bq", 2), ("bk", 2), ("bv", 2), ("b1_1", 8),
                  ("even", 1), ("odd", 1)):
    COLS[_name] = (sum(n for _, n in COLS.values()), _n)
NCOLS = sum(n for _, n in COLS.values())
ROWS = ("bproj_0", "bproj_1", "b2_0", "b2_1", "bada_gt_a", "bada_gt_m")


class Step:

    def __init__(self, attn, mlp, nxt, before_attn=None, before_mlp=None, late=False):
        self.attn, self.mlp, self.nxt = attn, mlp, nxt
        self.before_attn, self.before_mlp, self.late = before_attn, before_mlp, late


def even_step(i):
    return Step((2 * i - 1, 0, i), (2 * i - 2, 1, i - 2), (2 * i, 1, i - 1), (1, i - 2), (0, i - 1))


def odd_step(i, last=False):
    nxt = (2 * i + 1, 1, i) if last else (2 * i + 1, 0, i + 1)
    return Step((2 * i, 1, i - 1), (2 * i - 1, 0, i), nxt, (0, i), (1, i - 2), late=last)


def schedule(eng, step):
    step(Step((0, 0, 0), None, (1, 0, 1)))
    step(Step((1, 0, 1), (0, 0, 0), (2, 1, 0), (0, 0), None, late=True))
    step(Step((2, 1, 0), (1, 0, 1), (3, 0, 2), (0, 1), (0, 0)))
    with eng.Fori(2, NB - 1) as i:
        step(even_step(i))
        step(odd_step(i))
    step(even_step(NB - 1))
    step(odd_step(NB - 1, last=True))
    step(Step((2 * NB - 1, 1, NB - 1), (2 * NB - 2, 1, NB - 2), None, (1, NB - 2), (0, NB - 1)))
    step(Step(None, (2 * NB - 1, 1, NB - 1), None, (1, NB - 1), (1, NB - 2)))


def wait(eng, sem, value):
    if isinstance(value, int) and value <= 0:
        return
    eng.wait_ge(sem, value)


def build(nc, a, out):
    with ExitStack() as ctx:
        def sb(name, shape, dt=F32):
            return ctx.enter_context(nc.sbuf_tensor(name, shape, dt))

        def sem(name):
            return ctx.enter_context(nc.semaphore(name))

        def sems(name):
            return [sem(f"{name}_l0"), sem(f"{name}_l1")]

        ident = sb("ident", [P, P])
        identb = sb("identb", [P, P], BF16)
        causal = sb("causal", [P, S], BF16)
        cols = sb("cols", [P, NCOLS])
        rows = sb("rows", [P, len(ROWS), D])
        wqkv = [sb(f"wqkv{l}", [P, KT, 3 * D]) for l in range(2)]
        wproj = [sb(f"wproj{l}", [P, KT, D]) for l in range(2)]
        w1 = [sb(f"w1_{l}", [P, KT, MLP]) for l in range(2)]
        w2 = [sb(f"w2_{l}", [P, MC, D]) for l in range(2)]
        mod_mul = sb("mod_mul", [P, 2, 2, KT, NSEQ])
        mod_add = sb("mod_add", [P, 2, 2, KT, NSEQ])
        carrier = sb("carrier", [P, 1])
        bk_par = sb("bk_par", [P, 2])
        half_neg = sb("half_neg", [P, NT])
        condT = sb("condT", [P, KT, NSEQ])
        siluT = sb("siluT", [P, KT, NSEQ])
        col1 = sb("col1", [P, 8])
        gates = sb("gates", [NSEQ, 2, D])
        x_in = [sb("x_in", [P, NT, D]), sb("x_mid", [P, NT, D])]
        x_attn = [sb(f"x_attn{l}", [P, NT, D]) for l in range(2)]
        x_out = sb("x_out", [P, NT, D])
        mlp_dst = [x_in[1], x_out]
        gate_a = sb("gate_a", [P, NT, D])
        res_a = sb("res_a", [P, NT, D])
        xn_a = sb("xn_a", [P, NT, D])
        xmT_a = sb("xmT_a", [P, KT, BT])
        stats_a_buf = sb("stats_a", [P, NT, 6])
        mv_a = sb("mv_a", [P, NT, 2])
        ve_a = sb("ve_a", [P, NT])
        rstd_a = sb("rstd_a", [P, NT])
        qexp = sb("qexp", [P, KT, BS, PAIRS, S])
        kpar = sb("kpar", [P, KT, 2, BT])
        vals = sb("vals", [P, BS, PP, VW])
        probs = sb("probs", [P, 4, H // 2 * S])
        probsT = sb("probsT", [P, 2, H // 2 * S])
        row_max = sb("row_max", [P, 2, H // 2])
        recip = sb("recip", [P, 2, PP, 2])
        attn_n = sb("attn_n", [P, 2, PP, 2, HD])
        attnT = sb("attnT", [P, KT, BT])
        gated_a = sb("gated_a", [P, 2, D])
        pad_u8 = sb("pad_u8", [P, BT], U8)
        pad_bf = sb("pad_bf", [P, BT], BF16)
        gate_m = sb("gate_m", [P, NT, D])
        res_m = sb("res_m", [P, NT, D])
        xn_m = sb("xn_m", [P, NT, D])
        xmT_m = sb("xmT_m", [P, KT, BT])
        stats_m = sb("stats_m", [P, NT, 6])
        mv_m = sb("mv_m", [P, NT, 2])
        ve_m = sb("ve_m", [P, NT])
        rstd_m = sb("rstd_m", [P, NT])
        hid = sb("hid", [P, MC, BT])
        gated_m = sb("gated_m", [P, 2, D])
        tmp_mod = sb("tmp_mod", [P, 2, BT])
        wada = hid[:, 0:6, :].rearrange("p a b -> p (a b)").rearrange("p (k n) -> p k n", k=KT)
        wad1 = xmT_m[:, :, :].rearrange("p k n -> p (k n)").rearrange("p (k n) -> p k n", k=KT)
        wad2 = attnT[:, :, :].rearrange("p k n -> p (k n)").rearrange("p (k n) -> p k n", k=KT)
        bank_s = [ctx.enter_context(nc.psum_tensor(f"bank_s{i}", [P, 512], F32)) for i in range(2)]
        bank_t = [ctx.enter_context(nc.psum_tensor(f"bank_t{i}", [P, 512], F32)) for i in range(2)]
        bank_o = [ctx.enter_context(nc.psum_tensor(f"bank_o{i}", [P, 512], F32)) for i in range(2)]
        bank_l = [ctx.enter_context(nc.psum_tensor(f"bank_l{i}", [P, 512], F32)) for i in range(2)]
        gate_dram = nc.dram_tensor("gate_table", [2, NSEQ, D], F32, kind="Internal").ap()

        const_loaded, cond_loaded, cols_loaded = sem("const_loaded"), sem("cond_loaded"), sem("cols_loaded")
        rows_loaded, wada_loaded, wad1_loaded = sem("rows_loaded"), sem("wada_loaded"), sem("wad1_loaded")
        wqkv_loaded, wproj_loaded, w1_loaded, w2_loaded = sems("wqkv_loaded"), sems("wproj_loaded"), sems("w1_loaded"), sems("w2_loaded")
        zeroed, setup_dve, setup_exp = sem("zeroed"), sem("setup_dve"), sem("setup_exp")
        bk_ready, pool_const = sem("bk_ready"), sem("pool_const")
        silu_ready, mods_done, gates_done, fold_done = sem("silu_ready"), sem("mods_done"), sem("gates_done"), sem("fold_done")
        tables_ready, gates_ready = sem("tables_ready"), sem("gates_ready")
        x_loaded, gate_a_loaded, gate_m_loaded = sem("x_loaded"), sem("gate_a_loaded"), sem("gate_m_loaded")
        pad_loaded, pad_ready = sem("pad_loaded"), sem("pad_ready")
        stored = sem("stored")
        stats_done_a, var_done_a, rstd_done_a, xn_done_a = sem("stats_done_a"), sem("var_done_a"), sem("rstd_done_a"), sem("xn_done_a")
        aggr_done_a = sem("aggr_done_a")
        xnT_done_a, mod_mul_a, mod_add_a = sem("xnT_done_a"), sem("mod_mul_a"), sem("mod_add_a")
        qk_done, v_done = sem("qk_done"), sem("v_done")
        q_act, q_dve, k_act, k_dve = sem("q_by_act"), sem("q_by_dve"), sem("k_by_act"), sem("k_by_dve")
        v_act, v_dve = sem("v_by_act"), sem("v_by_dve")
        scores_done, max_done, shifted, probs_ready = sem("scores_done"), sem("max_done"), sem("shifted"), sem("probs_ready")
        probsT_done, probsT_ready, pv_done, recip_done = sem("probsT_done"), sem("probsT_ready"), sem("pv_done"), sem("recip_done")
        attn_n_ready, attn_nT_done, attnT_ready = sem("attn_n_ready"), sem("attn_nT_done"), sem("attnT_ready")
        proj_done = sem("proj_done")
        res_a_ready, attn_out = sems("res_a_ready"), sems("attn_out")
        proj_gated = sem("proj_gated")
        proj_read = [proj_gated, attn_out[1]]
        bias_a, bias_m = sem("gated_bias_a"), sem("gated_bias_m")
        stats_done_m, aggr_done_m, var_done_m, rstd_done_m, xn_done_m = sem("stats_done_m"), sem("aggr_done_m"), sem("var_done_m"), sem("rstd_done_m"), sem("xn_done_m")
        xnT_done_m, mod_mul_m, mod_add_m = sem("xnT_done_m"), sem("mod_mul_m"), sem("mod_add_m")
        up_done, gelu_done, down_done = sem("up_done"), sem("gelu_done"), sem("down_done")
        res_m_ready, mlp_out = sems("res_m_ready"), sems("mlp_out")
        down_gated = sem("down_gated")
        down_read = [down_gated, mlp_out[1]]

        x_v = a["x"].rearrange("(b t p) d -> b p t d", t=NT, p=P)
        out_v = out.rearrange("(b t p) d -> b p t d", t=NT, p=P)
        gate_v = gate_dram.rearrange("g (b t s) d -> g b s t d", t=NT, s=2)

        def col(name, k=0):
            at = COLS[name][0] + k
            return cols[:, at:at + 1]

        def row(name):
            return rows[:, ROWS.index(name), :]

        block = ctx.enter_context(nc.Block())

        @block.sync
        def _(sp):
            def load_x(b):
                sp.dma_start(x_in[0][:, :, :], x_v[b]).then_inc(x_loaded, 16)

            def load_gate(which, dst, b, loaded):
                for s in range(2):
                    src = gate_v[which, b, s]
                    sp.dma_start(dst[s * S:(s + 1) * S, :, :], src.unsqueeze(0).to_broadcast([S, NT, D])).then_inc(loaded, 8 * 2)

            def load_pad(at):
                sp.dma_start(pad_u8[:, :], a["pad"][bass.ds(at, BT)].unsqueeze(0).to_broadcast([P, BT])).then_inc(pad_loaded, 16)

            sp.dma_start(condT[:, :, :], a["condT"].rearrange("(k p) n -> p k n", p=P)).then_inc(cond_loaded, 16)
            sp.dma_start(cols[:, :], a["cols"]).then_inc(cols_loaded, 16)
            sp.dma_start(ident[:, :], a["ident"]).then_inc(const_loaded, 16)
            load_x(0)
            sp.dma_start(wada, a["wada"].rearrange("(k p) n -> p k n", p=P)).then_inc(wada_loaded, 16)
            sp.dma_start(wqkv[0][:, :, :], a["wqkv0"].rearrange("(k p) n -> p k n", p=P)).then_inc(wqkv_loaded[0], 16)
            sp.dma_start(identb[:, :], a["identb"]).then_inc(const_loaded, 16)
            sp.dma_start(causal[:, :], a["causal"]).then_inc(const_loaded, 16)
            sp.dma_start(rows[:, :, :], a["rows"].unsqueeze(0).to_broadcast([P, len(ROWS), D])).then_inc(rows_loaded, 16)
            sp.dma_start(wad1, a["wad1"].rearrange("(k p) n -> p k n", p=P)).then_inc(wad1_loaded, 16)
            sp.dma_start(wad2, a["wad2"].rearrange("(k p) n -> p k n", p=P)).then_inc(wad1_loaded, 16)
            for l in range(2):
                if l:
                    sp.dma_start(wqkv[l][:, :, :], a[f"wqkv{l}"].rearrange("(k p) n -> p k n", p=P)).then_inc(wqkv_loaded[l], 16)
                sp.dma_start(wproj[l][:, :, :], a[f"wproj{l}"].rearrange("(k p) n -> p k n", p=P)).then_inc(wproj_loaded[l], 16)
                sp.dma_start(w1[l][:, :, :], a[f"w1_{l}"].rearrange("(k p) n -> p k n", p=P)).then_inc(w1_loaded[l], 16)
                sp.dma_start(w2[l][:, :, :], a[f"w2_{l}"].rearrange("(k p) n -> p k n", p=P)).then_inc(w2_loaded[l], 16)
            sp.wait_ge(gates_ready, 2)
            sp.dma_start(gate_dram.rearrange("g s d -> s g d"), gates[:, :, :]).then_inc(stored, 16)
            sp.wait_ge(stored, 16)
            load_gate(0, gate_a, 0, gate_a_loaded)
            load_gate(1, gate_m, 0, gate_m_loaded)

            def step(st):
                if st.attn:
                    _, l, b = st.attn
                    more = not (isinstance(b, int) and b == NB - 1)
                    if st.nxt and st.nxt[1] == 1:
                        wait(sp, pad_ready, st.nxt[2])
                    if l == 0 and more:
                        wait(sp, res_a_ready[0], NT * (b + 1))
                        load_x(b + 1)
                    if st.nxt and st.nxt[1] == 1:
                        load_pad(st.nxt[2] * BT)
                if st.mlp:
                    _, lm, bm = st.mlp
                    if lm == 1:
                        wait(sp, mlp_out[1], NT * (bm + 1))
                        sp.dma_start(out_v[bm], x_out[:, :, :]).then_inc(stored, 16)
                if st.attn and l == 0 and more:
                    wait(sp, proj_gated, NT * (b + 1))
                    load_gate(0, gate_a, b + 1, gate_a_loaded)
                if st.mlp and lm == 0 and not (isinstance(bm, int) and bm == NB - 1):
                    wait(sp, down_gated, NT * (bm + 1))
                    load_gate(1, gate_m, bm + 1, gate_m_loaded)

            schedule(sp, step)
            sp.wait_ge(stored, 16 * (NB + 1))

        @block.tensor
        def _(pe):
            seen = set()

            def first_use(sem_, value=16):
                if sem_.name not in seen:
                    seen.add(sem_.name)
                    pe.wait_ge(sem_, value)

            def norm_transposes(which, n, xn, xn_done, done, banks, free):
                wait(pe, xn_done, NT * (n + 1))
                for k in range(KT):
                    free(k)
                    for t in range(NT):
                        mm = pe.transpose(banks[k][:, t * P:(t + 1) * P], xn[:, t, k * P:(k + 1) * P], ident[:, :])
                    mm.then_inc(done, 1)

            def transposes_a(n, l, b, after_step=None):
                def free(k):
                    if after_step is not None:
                        wait(pe, shifted, BS * after_step + 7 + k)
                norm_transposes("a", n, xn_a, xn_done_a, xnT_done_a, bank_s, free)

            def transposes_m(m):
                def free(k):
                    if m_before[0] is not None:
                        lp, bp = m_before[0]
                        wait(pe, down_read[lp], NT * bp + 3 + k)
                norm_transposes("m", m, xn_m, xn_done_m, xnT_done_m, bank_l, free)

            m_before = [None]

            def qkv(n, l):
                first_use(wqkv_loaded[l])
                wait(pe, mod_add_a, KT * (n + 1))
                wait(pe, mod_mul_a, KT * (n + 1))
                for j in range(KT):
                    for c in range(2):
                        if j == 1 and c == 0:
                            wait(pe, q_act, 4 * n + 2)
                            wait(pe, q_dve, 4 * n + 2)
                        if j == 1 and c == 1:
                            wait(pe, k_act, 2 * n + 2)
                        for k in range(KT):
                            at = c * D + j * P
                            mm = pe.matmul(bank_s[c][:, :], wqkv[l][:, k, at:at + P], xmT_a[:, k, :], start=(k == 0), stop=(k == KT - 1))
                        mm.then_inc(qk_done, 1)
                for t in range(NT):
                    if t == 0:
                        wait(pe, q_act, 4 * n + 4)
                        wait(pe, q_dve, 4 * n + 4)
                    elif t == 1:
                        wait(pe, k_dve, 2 * n + 2)
                    else:
                        wait(pe, v_act, 8 * n + 2 * (t - 1))
                        wait(pe, v_dve, 8 * n + 2 * (t - 1))
                    for k in range(KT):
                        mm = pe.matmul(bank_s[t % 2][:, 0:D], xmT_a[:, k, t * P:(t + 1) * P], wqkv[l][:, k, 2 * D:3 * D], start=(k == 0), stop=(k == KT - 1))
                    mm.then_inc(v_done, 1)

            def scores(n, l, b, s):
                if s == 0:
                    if l == 1:
                        wait(pe, pad_ready, b + 1)
                    wait(pe, q_act, 4 * n + 4)
                    wait(pe, k_dve, 2 * n + 2)
                if s < 2:
                    wait(pe, v_act, 8 * n + 6 + 2 * s)
                    wait(pe, v_dve, 8 * n + 6 + 2 * s)
                else:
                    wait(pe, shifted, BS * n + s - 1)
                bank = bank_s[s % 2]
                mask = causal[:, :] if l == 0 else pad_bf[:, s * S:(s + 1) * S]
                pe.matmul(bank[:, :].rearrange("p (g k) -> p g k", k=S), identb[:, :], mask.unsqueeze(1).to_broadcast([P, H // 2, S]), start=True, stop=False)
                for j in range(KT):
                    for u in range(2):
                        pp = 2 * j + u
                        mm = pe.matmul(bank[:, pp * P:(pp + 1) * P].rearrange("p (e k) -> p e k", e=2), qexp[:, j, s, 2 * u:2 * u + 2, :].rearrange("p a q -> p (a q)"),
                                       kpar[:, j, :, s * S:(s + 1) * S], start=False, stop=(pp == PP - 1))
                mm.then_inc(scores_done, 1)

            def probs_transposes(n, s):
                wait(pe, probs_ready, BS * n + s + 1)
                wait(pe, probsT_ready, BS * n + s - 1)
                for pp in range(PP):
                    mm = pe.transpose(bank_t[s % 2][:, pp * P:(pp + 1) * P], probs[:, s % 4, pp * P:(pp + 1) * P], ident[:, :])
                mm.then_inc(probsT_done, 1)

            def pv(n, l, s, before):
                if s == 0:
                    wait(pe, v_act, 8 * n + 8)
                    wait(pe, v_dve, 8 * n + 8)
                wait(pe, probsT_ready, BS * n + s + 1)
                wait(pe, attnT_ready, BS * n + s - 1)
                if s % 2 == 0:
                    if s >= 2:
                        wait(pe, proj_read[l], NT * before[2] + s // 2)
                    elif before[0] is not None:
                        wait(pe, proj_read[before[0]], NT * (before[1] + 1))
                for pp in range(PP):
                    mm = pe.matmul(bank_o[s % 2][:, pp * VW:(pp + 1) * VW], probsT[:, s % 2, pp * P:(pp + 1) * P], vals[:, s, pp, :], start=True, stop=True)
                mm.then_inc(pv_done, 1)

            def attn_transpose(n, s):
                wait(pe, attn_n_ready, 16 * n + 2 * s + 2)
                pe.transpose(bank_o[s % 2][:, OT0:OT0 + P], attn_n[:, s % 2, :, :, :].rearrange("p a e d -> p (a e d)"), ident[:, :]).then_inc(attn_nT_done, 1)

            def project(n, l, t):
                first_use(wproj_loaded[l])
                wait(pe, attnT_ready, BS * n + 2 * t + 2)
                for k in range(KT):
                    mm = pe.matmul(bank_o[0][:, 0:D], attnT[:, k, t * P:(t + 1) * P], wproj[l][:, k, :], start=(k == 0), stop=(k == KT - 1))
                mm.then_inc(proj_done, 1)

            def up(m, l, c):
                first_use(w1_loaded[l])
                if c == 0:
                    wait(pe, mod_add_m, KT * (m + 1))
                    wait(pe, mod_mul_m, KT * (m + 1))
                if c >= 2:
                    wait(pe, gelu_done, MC * m + c - 1)
                for k in range(KT):
                    mm = pe.matmul(bank_l[c % 2][:, :], w1[l][:, k, c * P:(c + 1) * P], xmT_m[:, k, :], start=(k == 0), stop=(k == KT - 1))
                mm.then_inc(up_done, 1)

            def down(m, l, b, t, halves=(0, 1)):
                first_use(w2_loaded[l])
                if 0 in halves:
                    if t < 2:
                        wait(pe, gelu_done, MC * (m + 1))
                    else:
                        wait(pe, down_read[l], NT * b + t - 1)
                for half in halves:
                    for c in range(half * MC // 2, (half + 1) * MC // 2):
                        mm = pe.matmul(bank_l[t % 2][:, 0:D], hid[:, c, t * P:(t + 1) * P], w2[l][:, c, :], start=(c == 0), stop=(c == MC - 1))
                if 1 in halves:
                    mm.then_inc(down_done, 1)

            pe.wait_ge(silu_ready, 1)
            pe.wait_ge(wada_loaded, 16)
            for which, at in enumerate((1, 0, 4, 3)):
                for j in range(KT):
                    for k in range(KT):
                        c0 = at * D + j * P
                        o0 = (which * KT + j) * NSEQ
                        mm = pe.matmul(bank_s[0][:, o0:o0 + NSEQ], wada[:, k, c0:c0 + P], siluT[:, k, :], start=(k == 0), stop=(k == KT - 1))
            mm.then_inc(mods_done, 1)
            for g, at in enumerate((2, 5)):
                for k in range(KT):
                    mm = pe.matmul(bank_t[0][0:NSEQ, g * D:(g + 1) * D], siluT[:, k, :], wada[:, k, at * D:(at + 1) * D], start=(k == 0), stop=(k == KT - 1))
            mm.then_inc(gates_done, 1)
            pe.wait_ge(wad1_loaded, 32)
            for which in range(4):
                w = (wad1, wad2)[which // 2]
                for j in range(KT):
                    for k in range(KT):
                        c0 = (which % 2) * D + j * P
                        o0 = (which * KT + j) * NSEQ
                        mm = pe.matmul(bank_l[0][:, o0:o0 + NSEQ], w[:, k, c0:c0 + P], condT[:, k, :], start=(k == 0), stop=(k == KT - 1))
            mm.then_inc(mods_done, 1)
            pe.wait_ge(const_loaded, 48)
            pe.wait_ge(tables_ready, 1)
            transposes_a(0, 0, 0)

            def step(st):
                m_before[0] = st.before_mlp
                if st.attn:
                    n, l, b = st.attn
                    before = (*(st.before_attn or (None, None)), b)
                    qkv(n, l)
                if st.mlp:
                    m, lm, bm = st.mlp
                    if isinstance(m, int) and m == 0:
                        pe.wait_ge(tables_ready, 2)
                    transposes_m(m)
                if not st.attn:
                    for c in range(MC):
                        up(m, lm, c)
                    for t in range(NT):
                        down(m, lm, bm, t)
                    return
                for s in (0, 1):
                    scores(n, l, b, s)
                if isinstance(n, int) and n == 0:
                    first_use(wproj_loaded[1])
                    for k in range(KT):
                        mm = pe.matmul(bank_l[1][:, 0:D], bv_wide[:, k, :], wproj[1][:, k, :], start=(k == 0), stop=(k == KT - 1))
                    mm.then_inc(fold_done, 1)
                if st.mlp:
                    for c in range(MC // 2):
                        up(m, lm, c)
                for g in range(1, BS // 2):
                    for s in (2 * g, 2 * g + 1):
                        scores(n, l, b, s)
                    for s in (2 * g - 2, 2 * g - 1):
                        probs_transposes(n, s)
                    if st.mlp:
                        if g == 1:
                            up(m, lm, 4)
                            up(m, lm, 5)
                        else:
                            down(m, lm, bm, 2 * g - 4, (0, 1) if g == 2 else (0,))
                    for s in (2 * g - 2, 2 * g - 1):
                        pv(n, l, s, before)
                    if st.mlp:
                        if g == 1:
                            up(m, lm, 6)
                        elif g == 2:
                            down(m, lm, bm, 1, (0,))
                        else:
                            down(m, lm, bm, 2, (1,))
                    for s in (2 * g - 2, 2 * g - 1):
                        attn_transpose(n, s)
                    if st.mlp:
                        if g == 1:
                            up(m, lm, 7)
                        elif g == 2:
                            down(m, lm, bm, 1, (1,))
                    project(n, l, g - 1)
                for s in (6, 7):
                    probs_transposes(n, s)
                if st.mlp:
                    down(m, lm, bm, 3, (0,))
                for s in (6, 7):
                    pv(n, l, s, before)
                if st.mlp:
                    down(m, lm, bm, 3, (1,))
                if st.nxt:
                    transposes_a(st.nxt[0], st.nxt[1], st.nxt[2], after_step=n)
                for s in (6, 7):
                    attn_transpose(n, s)
                project(n, l, 3)

            bv_wide = cols[:, COLS["bv"][0]:COLS["bv"][0] + KT].unsqueeze(2).to_broadcast([P, KT, P])
            pe.wait_ge(cols_loaded, 16)
            pe.wait_ge(zeroed, 3)
            schedule(pe, step)

        @block.vector
        def _(dve):
            def stats(n, x, arrived, st_, mv, ve, done, aggr, var, read):
                for t in range(NT):
                    arrived(t)
                    dve.bn_stats(st_[:, t, :], x[:, t, :]).then_inc(done, 1)
                wait(dve, done, NT * (n + 1))
                wait(dve, read, NT * n)
                dve.memset(carrier[:, :], 0.0)
                for t in range(NT):
                    dve.bn_aggr(mv[:, t, :], st_[:, t, :]).then_inc(aggr, 1)
                wait(dve, aggr, NT * (n + 1))
                dve.tensor_scalar(ve[:, :], mv[:, :, 1], EPS, None, ALU.add).then_inc(var, 1)

            def normalise(n, x, mv, rstd, xn, rstd_done, xnT_done, done):
                wait(dve, rstd_done, n + 1)
                wait(dve, xnT_done, KT * n)
                for t in range(NT):
                    dve.tensor_scalar(xn[:, t, :], x[:, t, :], mv[:, t, 0:1], rstd[:, t:t + 1], ALU.subtract, ALU.mult).then_inc(done, 1)

            def modulate(n, l, b, norm, banks, xmT, xnT_done, mul, add):
                for k in range(KT):
                    wait(dve, xnT_done, KT * n + k + 1)
                    if norm == 1:
                        wait(dve, up_done, MC * n)
                    else:
                        wait(dve, v_done, NT * n)
                    src = banks[k][:, :].rearrange("p (s q) -> p s q", q=S)
                    tmp = tmp_mod[:, k, :].rearrange("p (s q) -> p s q", q=S)
                    factor = mod_mul[:, l, norm, k, bass.ds(BS * b, BS)].unsqueeze(2).to_broadcast([P, BS, S])
                    dve.tensor_tensor(tmp, src, factor, ALU.mult).then_inc(mul, 1)
                for k in range(KT):
                    wait(dve, mul, KT * n + k + 1)
                    tmp = tmp_mod[:, k, :].rearrange("p (s q) -> p s q", q=S)
                    term = mod_add[:, l, norm, k, bass.ds(BS * b, BS)].unsqueeze(2).to_broadcast([P, BS, S])
                    dve.tensor_tensor(xmT[:, k, :].rearrange("p (s q) -> p s q", q=S), tmp, term, ALU.add).then_inc(add, 1)

            def stats_a(n, l, b):
                def arrived(t):
                    if l == 0:
                        wait(dve, x_loaded, 16 * (b + 1))
                    else:
                        wait(dve, mlp_out[0], NT * b + t + 1)
                stats(n, x_in[l], arrived, stats_a_buf, mv_a, ve_a, stats_done_a, aggr_done_a, var_done_a, xn_done_a)

            def normalise_a(n, l):
                normalise(n, x_in[l], mv_a, rstd_a, xn_a, rstd_done_a, xnT_done_a, xn_done_a)

            def modulate_a(n, l, b):
                modulate(n, l, b, 0, bank_s, xmT_a, xnT_done_a, mod_mul_a, mod_add_a)

            def stats_mlp(m, l, b):
                stats(m, x_attn[l], lambda t: wait(dve, attn_out[l], NT * b + t + 1), stats_m, mv_m, ve_m, stats_done_m, aggr_done_m, var_done_m, xn_done_m)

            def normalise_mlp(m, l):
                normalise(m, x_attn[l], mv_m, rstd_m, xn_m, rstd_done_m, xnT_done_m, xn_done_m)

            def queries(n, l, j):
                wait(dve, qk_done, 4 * n + 2 * j + 1)
                wait(dve, scores_done, BS * n)
                for pr in (2, 3):
                    r = slice(32 * pr, 32 * pr + 32)
                    dst, src = qexp[r, j, :, pr, :], bank_s[0][r, :].rearrange("p (s q) -> p s q", q=S)
                    if l == 0:
                        i = dve.tensor_copy(dst, src)
                    else:
                        i = dve.tensor_scalar(dst, src, cols[r, COLS["bq"][0] + j:COLS["bq"][0] + j + 1], None, ALU.add)
                    i.then_inc(q_dve, 1)

            def keys(n, l):
                wait(dve, qk_done, 4 * n + 4)
                for e, name in enumerate(("even", "odd")):
                    if l == 0:
                        i = dve.tensor_scalar(kpar[:, 1, e, :], bank_s[1][:, :], col(name), None, ALU.mult)
                    else:
                        i = dve.tensor_scalar(kpar[:, 1, e, :], bank_s[1][:, :], col("bk", 1), col(name), ALU.add, ALU.mult)
                    i.then_inc(k_dve, 1)

            def values(n, t):
                wait(dve, v_done, NT * n + t + 1)
                wait(dve, pv_done, BS * n)
                src = bank_s[t % 2][S:2 * S, 0:D].rearrange("p (a b e d) -> p a b e d", a=PP, b=2, e=2)
                for e in range(2):
                    dst = vals[e * S:(e + 1) * S, 2 * t + 1, :, 0:4 * HD].rearrange("p a (b e d) -> p a b e d", b=2, e=2)
                    dve.tensor_copy(dst[:, :, :, e, :], src[:, :, :, e, :]).then_inc(v_dve, 1)

            def pad_mask(n, b):
                wait(dve, pad_loaded, 16 * (b + 1))
                wait(dve, scores_done, BS * n)
                dve.tensor_scalar(pad_bf[:, :], pad_u8[:, :], MASKED, None, ALU.mult).then_inc(pad_ready, 1)

            def shift(n, s):
                bank = bank_s[s % 2][:, :].rearrange("p (g k) -> p g k", k=S)
                wait(dve, scores_done, BS * n + s + 1)
                dve.tensor_reduce(row_max[:, s % 2, :], bank, AX.X, ALU.max).then_inc(max_done, 1)
                wait(dve, max_done, BS * n + s + 1)
                wait(dve, probsT_done, BS * n + s - 3)
                dve.tensor_tensor(probs[:, s % 4, :].rearrange("p (g k) -> p g k", k=S), bank, row_max[:, s % 2, :].unsqueeze(2).to_broadcast([P, H // 2, S]),
                                  ALU.subtract).then_inc(shifted, 1)

            def divide(n, s):
                bank = bank_o[s % 2][:, 0:PP * VW].rearrange("p (a w) -> p a w", a=PP)
                wait(dve, pv_done, BS * n + s + 1)
                dve.reciprocal(recip[:, s % 2, :, :], bank[:, :, 4 * HD:4 * HD + 2]).then_inc(recip_done, 1)
                wait(dve, recip_done, BS * n + s + 1)
                wait(dve, attn_nT_done, BS * n + s - 1)
                for b in range(2):
                    r = slice(b * S, (b + 1) * S)
                    src = bank[r, :, b * 2 * HD:(b + 1) * 2 * HD].rearrange("p a (e d) -> p a e d", e=2)
                    dve.tensor_tensor(attn_n[r, s % 2, :, :, :], src, recip[r, s % 2, :, :].unsqueeze(3).to_broadcast([S, PP, 2, HD]), ALU.mult).then_inc(attn_n_ready, 1)

            def add_projection(n, l, b, t):
                wait(dve, proj_done, NT * n + t + 1)
                if l == 0:
                    wait(dve, gate_a_loaded, 32 * (b + 1))
                    dve.tensor_tensor(gated_a[:, t % 2, :], bank_o[0][:, 0:D], gate_a[:, t, :], ALU.mult).then_inc(proj_gated, 1)
                    wait(dve, proj_gated, NT * b + t + 1)
                    src = gated_a[:, t % 2, :]
                else:
                    src = bank_o[0][:, 0:D]
                wait(dve, res_a_ready[l], NT * b + t + 1)
                wait(dve, res_m_ready[l], NT * b)
                dve.tensor_tensor(x_attn[l][:, t, :], src, res_a[:, t, :], ALU.add).then_inc(attn_out[l], 1)

            def add_down(m, l, b, t):
                wait(dve, down_done, NT * m + t + 1)
                if l == 0:
                    wait(dve, gate_m_loaded, 32 * (b + 1))
                    dve.tensor_tensor(gated_m[:, t % 2, :], bank_l[t % 2][:, 0:D], gate_m[:, t, :], ALU.mult).then_inc(down_gated, 1)
                    wait(dve, down_gated, NT * b + t + 1)
                    src = gated_m[:, t % 2, :]
                    wait(dve, res_a_ready[1], NT * b)
                else:
                    src = bank_l[t % 2][:, 0:D]
                    wait(dve, stored, 16 * (b + 1))
                wait(dve, res_m_ready[l], NT * b + t + 1)
                dve.tensor_tensor(mlp_dst[l][:, t, :], src, res_m[:, t, :], ALU.add).then_inc(mlp_out[l], 1)

            dve.memset(qexp[:, :, :, :, :], 0.0).then_inc(zeroed, 1)
            dve.memset(vals[:, :, :, :], 0.0).then_inc(zeroed, 1)
            dve.wait_ge(setup_exp, 1)
            dve.tensor_scalar(siluT[:, :, :], siluT[:, :, :], 1.0, None, ALU.add).then_inc(setup_dve, 1)
            dve.wait_ge(setup_dve, 1)
            dve.reciprocal(siluT[:, :, :], siluT[:, :, :]).then_inc(setup_dve, 1)
            dve.wait_ge(setup_dve, 2)
            dve.tensor_tensor(siluT[:, :, :], siluT[:, :, :], condT[:, :, :], ALU.mult).then_inc(silu_ready, 1)
            dve.wait_ge(zeroed, 2)
            for e in range(2):
                i = dve.memset(vals[e * S:(e + 1) * S, :, :, 4 * HD + e:4 * HD + e + 1], 1.0)
            i.then_inc(zeroed, 1)
            stats_a(0, 0, 0)
            normalise_a(0, 0)
            dve.wait_ge(cols_loaded, 16)
            for i, name in enumerate(("bada_sc_a", "bada_sc_m", "sc1_1", "sc2_1")):
                at = COLS[name][0]
                dve.tensor_scalar(col1[:, 2 * i:2 * i + 2], cols[:, at:at + 2], 1.0, None, ALU.add).then_inc(setup_dve, 1)
            dve.wait_ge(setup_dve, 6)
            dve.wait_ge(mods_done, 1)
            n_tab = 6
            for norm, (g, be, sh) in enumerate((("g1", "be1", "bada_sh_a"), ("g2", "be2", "bada_sh_m"))):
                for k in range(KT):
                    sc_ps = bank_s[0][:, (2 * norm * KT + k) * NSEQ:(2 * norm * KT + k + 1) * NSEQ]
                    sh_ps = bank_s[0][:, ((2 * norm + 1) * KT + k) * NSEQ:((2 * norm + 1) * KT + k + 1) * NSEQ]
                    one = col1[:, 2 * norm + k:2 * norm + k + 1]
                    dve.tensor_scalar(mod_mul[:, 0, norm, k, :], sc_ps, one, col(g, k), ALU.add, ALU.mult).then_inc(setup_dve, 1)
                    dve.tensor_scalar(tmp_mod[:, k, norm * NSEQ:(norm + 1) * NSEQ], sc_ps, one, col(be, k), ALU.add, ALU.mult).then_inc(setup_dve, 1)
                    n_tab += 2
                    dve.wait_ge(setup_dve, n_tab)
                    i = dve.scalar_tensor_tensor(out=mod_add[:, 0, norm, k, :], in0=sh_ps, scalar=col(sh, k), in1=tmp_mod[:, k, norm * NSEQ:(norm + 1) * NSEQ],
                                                 op0=ALU.add, op1=ALU.add)
            i.then_inc(tables_ready, 1)
            dve.wait_ge(tables_ready, 1)
            modulate_a(0, 0, 0)
            dve.wait_ge(gates_done, 1)
            dve.wait_ge(rows_loaded, 16)
            for g, name in enumerate(("bada_gt_a", "bada_gt_m")):
                dve.tensor_tensor(gates[:, g, :], bank_t[0][0:NSEQ, g * D:(g + 1) * D], rows[0:NSEQ, ROWS.index(name), :], ALU.add).then_inc(gates_ready, 1)
            dve.wait_ge(mods_done, 2)
            for norm, sh in enumerate(("sh1_1", "sh2_1")):
                for k in range(KT):
                    sc_ps = bank_l[0][:, (2 * norm * KT + k) * NSEQ:(2 * norm * KT + k + 1) * NSEQ]
                    sh_ps = bank_l[0][:, ((2 * norm + 1) * KT + k) * NSEQ:((2 * norm + 1) * KT + k + 1) * NSEQ]
                    dve.tensor_scalar(mod_mul[:, 1, norm, k, :], sc_ps, col1[:, 4 + 2 * norm + k:5 + 2 * norm + k], None, ALU.add)
                    i = dve.tensor_scalar(mod_add[:, 1, norm, k, :], sh_ps, col(sh, k), None, ALU.add)
            i.then_inc(tables_ready, 1)
            dve.wait_ge(tables_ready, 2)

            def step(st):
                if st.mlp:
                    m, lm, bm = st.mlp
                if not st.attn:
                    stats_mlp(m, lm, bm)
                    normalise_mlp(m, lm)
                    modulate(m, lm, bm, 1, bank_l, xmT_m, xnT_done_m, mod_mul_m, mod_add_m)
                    for t in range(NT):
                        add_down(m, lm, bm, t)
                    return
                n, l, b = st.attn
                queries(n, l, 0)
                if l == 1:
                    pad_mask(n, b)
                if st.mlp:
                    stats_mlp(m, lm, bm)
                queries(n, l, 1)
                keys(n, l)
                if st.mlp:
                    normalise_mlp(m, lm)
                for t in range(NT):
                    values(n, t)
                if st.mlp:
                    modulate(m, lm, bm, 1, bank_l, xmT_m, xnT_done_m, mod_mul_m, mod_add_m)
                shift(n, 0)
                shift(n, 1)
                if isinstance(n, int) and n == 0:
                    dve.wait_ge(fold_done, 1)
                    dve.tensor_tensor(row("bproj_1"), bank_l[1][:, 0:D], row("bproj_1"), ALU.add).then_inc(tables_ready, 1)
                for g in range(1, BS // 2):
                    shift(n, 2 * g)
                    shift(n, 2 * g + 1)
                    if g == 2 and st.nxt and not st.late:
                        stats_a(*st.nxt)
                    if g == 3 and st.nxt and not st.late:
                        normalise_a(st.nxt[0], st.nxt[1])
                    if st.mlp and g == 2:
                        add_down(m, lm, bm, 0)
                    divide(n, 2 * g - 2)
                    divide(n, 2 * g - 1)
                    if st.mlp and g >= 2:
                        add_down(m, lm, bm, g - 1)
                    add_projection(n, l, b, g - 1)
                divide(n, 6)
                divide(n, 7)
                if st.mlp:
                    add_down(m, lm, bm, 3)
                if st.nxt:
                    if st.late:
                        stats_a(*st.nxt)
                        normalise_a(st.nxt[0], st.nxt[1])
                    modulate_a(*st.nxt)
                add_projection(n, l, b, 3)

            schedule(dve, step)

        @block.scalar
        def _(act):
            def queries(n, l, j):
                wait(act, qk_done, 4 * n + 2 * j + 1)
                wait(act, scores_done, BS * n)
                for pr in (0, 1):
                    r = slice(32 * pr, 32 * pr + 32)
                    bias = 0.0 if l == 0 else cols[r, COLS["bq"][0] + j:COLS["bq"][0] + j + 1]
                    act.activation(qexp[r, j, :, pr, :], bank_s[0][r, :].rearrange("p (s q) -> p s q", q=S), ACT.Identity, bias=bias).then_inc(q_act, 1)

            def keys(n, l):
                wait(act, qk_done, 4 * n + 2)
                for e, name in enumerate(("even", "odd")):
                    bias = 0.0 if l == 0 else bk_par[:, e:e + 1]
                    act.activation(kpar[:, 0, e, :], bank_s[1][:, :], ACT.Identity, bias=bias, scale=col(name)).then_inc(k_act, 1)

            def values(n, t):
                wait(act, v_done, NT * n + t + 1)
                wait(act, pv_done, BS * n)
                src = bank_s[t % 2][0:S, 0:D].rearrange("p (a b e d) -> p a b e d", a=PP, b=2, e=2)
                for e in range(2):
                    dst = vals[e * S:(e + 1) * S, 2 * t, :, 0:4 * HD].rearrange("p a (b e d) -> p a b e d", b=2, e=2)
                    act.activation(dst[:, :, :, e, :], src[:, :, :, e, :], ACT.Copy).then_inc(v_act, 1)

            def exps(n, s):
                wait(act, shifted, BS * n + s + 1)
                act.activation(probs[:, s % 4, :], probs[:, s % 4, :], ACT.Exp, scale=SCALE).then_inc(probs_ready, 1)

            def read_probsT(n, s):
                wait(act, probsT_done, BS * n + s + 1)
                wait(act, pv_done, BS * n + s - 1)
                act.activation(probsT[:, s % 2, :], bank_t[s % 2][:, :], ACT.Copy).then_inc(probsT_ready, 1)

            def read_attnT(n, s):
                wait(act, attn_nT_done, BS * n + s + 1)
                if s == 0:
                    wait(act, proj_done, NT * n)
                act.activation(attnT[:, :, s * S:(s + 1) * S], bank_o[s % 2][:, OT0:OT0 + P].rearrange("p (k q) -> p k q", k=KT), ACT.Copy).then_inc(attnT_ready, 1)

            def gelu(m, l, c):
                wait(act, up_done, MC * m + c + 1)
                if c == 0:
                    wait(act, down_done, NT * m)
                act.activation(hid[:, c, :], bank_l[c % 2][:, :], ACT.Gelu, bias=col(f"b1_{l}", c)).then_inc(gelu_done, 1)

            act.wait_ge(cond_loaded, 16)
            act.activation(siluT[:, :, :], condT[:, :, :], ACT.Exp, scale=-1.0).then_inc(setup_exp, 1)
            act.wait_ge(cols_loaded, 16)
            for e, name in enumerate(("even", "odd")):
                act.activation(bk_par[:, e:e + 1], col("bk"), ACT.Identity, scale=col(name)).then_inc(bk_ready, 1)
            act.wait_ge(bk_ready, 2)
            act.wait_ge(zeroed, 3)

            def step(st):
                if st.mlp:
                    m, lm, bm = st.mlp
                if not st.attn:
                    for c in range(MC):
                        gelu(m, lm, c)
                    return
                n, l, b = st.attn
                queries(n, l, 0)
                keys(n, l)
                queries(n, l, 1)
                for t in range(NT):
                    values(n, t)
                exps(n, 0)
                exps(n, 1)
                if st.mlp:
                    for c in range(MC // 2):
                        gelu(m, lm, c)
                for g in range(1, BS // 2):
                    read_probsT(n, 2 * g - 2)
                    read_probsT(n, 2 * g - 1)
                    exps(n, 2 * g)
                    exps(n, 2 * g + 1)
                    if st.mlp and g == 1:
                        for c in (4, 5, 6):
                            gelu(m, lm, c)
                    read_attnT(n, 2 * g - 2)
                    read_attnT(n, 2 * g - 1)
                    if st.mlp and g == 1:
                        gelu(m, lm, 7)
                read_probsT(n, 6)
                read_probsT(n, 7)
                read_attnT(n, 6)
                read_attnT(n, 7)

            schedule(act, step)

        @block.gpsimd
        def _(pool):
            def rstd(n, ve, out_, var, xn_done, done):
                wait(pool, var, n + 1)
                wait(pool, xn_done, NT * n)
                pool.tensor_tensor(out_[:, :], ve[:, :], half_neg[:, :], ALU.pow).then_inc(done, 1)

            def residual(l, b, kind, before):
                x, res, gate, loaded, ready, gated, bias = (
                    (x_in[l], res_a, gate_a, gate_a_loaded, res_a_ready, bias_a, row(f"bproj_{l}")) if kind == "a" else
                    (x_attn[l], res_m, gate_m, gate_m_loaded, res_m_ready, bias_m, row(f"b2_{l}")))
                if before:
                    wait(pool, (attn_out if kind == "a" else mlp_out)[before[0]], NT * (before[1] + 1))
                if l == 0:
                    wait(pool, loaded, 32 * (b + 1))
                    for t in range(NT):
                        pool.tensor_tensor(res[:, t, :], gate[:, t, :], bias, ALU.mult).then_inc(gated, 1)
                    wait(pool, gated, NT * (b + 1))
                if kind == "a" and l == 0:
                    wait(pool, x_loaded, 16 * (b + 1))
                elif kind == "a":
                    wait(pool, mlp_out[0], NT * (b + 1))
                else:
                    wait(pool, attn_out[l], NT * (b + 1))
                for t in range(NT):
                    pool.tensor_tensor(res[:, t, :], x[:, t, :], res[:, t, :] if l == 0 else bias, ALU.add).then_inc(ready[l], 1)

            pool.memset(half_neg[:, :], -0.5).then_inc(pool_const, 1)
            pool.wait_ge(pool_const, 1)
            rstd(0, ve_a, rstd_a, var_done_a, xn_done_a, rstd_done_a)
            pool.wait_ge(rows_loaded, 16)

            def step(st):
                if st.mlp:
                    m, lm, bm = st.mlp
                    rstd(m, ve_m, rstd_m, var_done_m, xn_done_m, rstd_done_m)
                if st.attn:
                    if isinstance(st.attn[0], int) and st.attn[0] == 2:
                        pool.wait_ge(tables_ready, 3)
                    residual(st.attn[1], st.attn[2], "a", st.before_attn)
                if st.mlp:
                    residual(lm, bm, "m", st.before_mlp)
                if st.nxt:
                    rstd(st.nxt[0], ve_a, rstd_a, var_done_a, xn_done_a, rstd_done_a)

            schedule(pool, step)


def layer_columns(v):
    return np.asarray(v).reshape(-1, P).T


def by_pair_parity(w):
    w = np.asarray(w)
    return w.reshape(PP, 2, 2 * HD, -1).transpose(1, 0, 2, 3).reshape(w.shape)


def kernel(**inputs):
    import concourse.bacc as bacc
    from concourse.bass_utils import run_bass_kernel_spmd

    v = {k: np.asarray(x) for k, x in inputs.items()}
    L0 = {k[8:]: x for k, x in v.items() if k.startswith("L0_cond_")}
    L1 = {k[8:]: x for k, x in v.items() if k.startswith("L1_cond_")}
    f32 = np.float32
    even = (np.arange(P) // HD % 2 == 0).astype(f32)
    bada, ad1, ad2 = L0["bada"].reshape(6, D), L1["b_adaln1"].reshape(2, D), L1["b_adaln2"].reshape(2, D)
    vectors = {
        "g1": L0["g1"], "be1": L0["be1"], "g2": L0["g2"], "be2": L0["be2"],
        "bada_sc_a": bada[1], "bada_sh_a": bada[0], "bada_sc_m": bada[4], "bada_sh_m": bada[3], "b1_0": L0["b1"],
        "sc1_1": ad1[0], "sh1_1": ad1[1], "sc2_1": ad2[0], "sh2_1": ad2[1],
        "bq": L1["bq"], "bk": L1["bk"], "bv": by_pair_parity(L1["bv"]), "b1_1": L1["b1"],
        "even": even, "odd": np.where(even > 0, f32(0), f32(1)),
    }
    bf16 = mybir.dt.np(BF16)
    q, k = np.arange(P)[:, None] % S, np.arange(S)[None, :]
    arrays = {
        "x": v["x"].reshape(NSEQ * S, D),
        "pad": v["mask_BxS_bf0"].reshape(-1),
        "condT": v["cond_1024"].T,
        "cols": np.concatenate([layer_columns(vectors[name]) for name in COLS], axis=1),
        "rows": np.stack([L0["bproj"], L1["bo"], L0["b2"], L1["b2"], bada[2], bada[5]]),
        "ident": np.eye(P, dtype=f32),
        "identb": np.eye(P, dtype=f32).astype(bf16),
        "causal": np.where(k <= q, 0.0, MASKED).astype(bf16),
        "wada": L0["Wada"],
        "wad1": L1["w_adaln1"].T, "wad2": L1["w_adaln2"].T,
        "wqkv0": L0["Wqkv"], "wqkv1": np.concatenate([L1["wq"].T, L1["wk"].T, L1["wv"].T], axis=1),
        "wproj0": by_pair_parity(L0["Wproj"]), "wproj1": by_pair_parity(L1["wo"].T),
        "w1_0": L0["W1"], "w1_1": L1["w1"].T,
        "w2_0": L0["W2"], "w2_1": L1["w2"].T,
    }
    arrays = {k_: np.ascontiguousarray(x) for k_, x in arrays.items()}
    nc = bacc.Bacc("TRN2", target_bir_lowering=False, num_devices=1)
    aps = {k_: nc.dram_tensor(f"in_{k_}", x.shape, mybir.dt.from_np(x.dtype), kind="ExternalInput").ap() for k_, x in arrays.items()}
    out = nc.dram_tensor("out", (NSEQ * S, D), F32, kind="ExternalOutput").ap()
    build(nc, aps, out)
    r = run_bass_kernel_spmd(nc, [{f"in_{k_}": x for k_, x in arrays.items()}], core_ids=[0])
    return r.results[0]["out"].reshape(NSEQ, S, D)
```

```python
from contextlib import ExitStack

import numpy as np

import concourse.bass as bass
from concourse import mybir

F32 = mybir.dt.float32
F32R = mybir.dt.float32r
BF16 = mybir.dt.bfloat16
U8 = mybir.dt.uint8
ALU = mybir.AluOpType
ACT = mybir.ActivationFunctionType
AX = mybir.AxisListType

P = 128
NSEQ, S, D = 64, 64, 256
H, HD = 16, 16
MLP = 1024
BS = 8
NB = NSEQ // BS
BT = BS * S
NT = BT // P
KT = D // P
MC = MLP // P
PAIRS = P // (2 * HD)
PP = H // 4
VW = 4 * HD + 2
OT0 = 384
EPS = 1e-5
MASKED = -1e30
SCALE = HD ** -0.5
GROUP = 2

COLS = {}
for _name, _n in (("g1", 2), ("be1", 2), ("g2", 2), ("be2", 2), ("bada_sc_a", 2), ("bada_sh_a", 2),
                  ("bada_sc_m", 2), ("bada_sh_m", 2), ("b1_0", 8), ("sc1_1", 2), ("sh1_1", 2),
                  ("sc2_1", 2), ("sh2_1", 2), ("bq", 2), ("bk", 2), ("bv", 2), ("b1_1", 8),
                  ("even", 1), ("odd", 1)):
    COLS[_name] = (sum(n for _, n in COLS.values()), _n)
NCOLS = sum(n for _, n in COLS.values())
ROWS = ("bproj_0", "bproj_1", "b2_0", "b2_1", "bada_gt_a", "bada_gt_m")


class Step:

    def __init__(self, attn, mlp, nxt, before_attn=None, before_mlp=None, late=False):
        self.attn, self.mlp, self.nxt = attn, mlp, nxt
        self.before_attn, self.before_mlp, self.late = before_attn, before_mlp, late


def even_step(i):
    return Step((2 * i - 1, 0, i), (2 * i - 2, 1, i - 2), (2 * i, 1, i - 1), (1, i - 2), (0, i - 1))


def odd_step(i, last=False):
    nxt = (2 * i + 1, 1, i) if last else (2 * i + 1, 0, i + 1)
    return Step((2 * i, 1, i - 1), (2 * i - 1, 0, i), nxt, (0, i), (1, i - 2), late=last)


def schedule(eng, step):
    step(Step((0, 0, 0), None, (1, 0, 1)))
    step(Step((1, 0, 1), (0, 0, 0), (2, 1, 0), (0, 0), None, late=True))
    step(Step((2, 1, 0), (1, 0, 1), (3, 0, 2), (0, 1), (0, 0)))
    with eng.Fori(2, NB - 1) as i:
        step(even_step(i))
        step(odd_step(i))
    step(even_step(NB - 1))
    step(odd_step(NB - 1, last=True))
    step(Step((2 * NB - 1, 1, NB - 1), (2 * NB - 2, 1, NB - 2), None, (1, NB - 2), (0, NB - 1)))
    step(Step(None, (2 * NB - 1, 1, NB - 1), None, (1, NB - 1), (1, NB - 2)))


def wait(eng, sem, value):
    if isinstance(value, int) and value <= 0:
        return
    eng.wait_ge(sem, value)


def build(nc, a, out):
    with ExitStack() as ctx:
        def sb(name, shape, dt=F32):
            return ctx.enter_context(nc.sbuf_tensor(name, shape, dt))

        def sem(name):
            return ctx.enter_context(nc.semaphore(name))

        def sems(name):
            return [sem(f"{name}_l0"), sem(f"{name}_l1")]

        ident = sb("ident", [P, P])
        identb = sb("identb", [P, P], BF16)
        causal = sb("causal", [P, S], BF16)
        cols = sb("cols", [P, NCOLS])
        rows = sb("rows", [P, len(ROWS), D])
        wqkv = [[sb(f"wqkv{l}_{part}", [P, KT, 3 * D], F32R) for part in ("hi", "lo")] for l in range(2)]
        wproj = [sb(f"wproj{l}", [P, KT, D]) for l in range(2)]
        w1 = [[sb(f"w1_{l}_{part}", [P, KT, MLP], F32R) for part in ("hi", "lo")] for l in range(2)]
        w2 = [sb(f"w2_{l}", [P, MC, D]) for l in range(2)]
        mod_mul = sb("mod_mul", [P, 2, 2, KT, NSEQ])
        mod_add = sb("mod_add", [P, 2, 2, KT, NSEQ])
        carrier = sb("carrier", [P, 1])
        gelu_carrier = sb("gelu_carrier", [P, 1])
        bk_par = sb("bk_par", [P, 2])
        half_neg = sb("half_neg", [P, NT])
        condT = sb("condT", [P, KT, NSEQ])
        siluT = sb("siluT", [P, KT, NSEQ])
        col1 = sb("col1", [P, 8])
        gates = sb("gates", [NSEQ, 2, D])
        x_in = [sb("x_in", [P, NT, D]), sb("x_mid", [P, NT, D])]
        x_attn = [sb(f"x_attn{l}", [P, NT, D]) for l in range(2)]
        xn = sb("xn", [P, NT, D])
        xm = [sb(f"xm_{part}", [P, KT, BT], F32R) for part in ("hi", "lo")]
        gate_bias = sb("gate_bias", [P, 2, D])
        gate_a = sb("gate_a", [P, NT, D])
        stats_a_buf = sb("stats_a", [P, NT, 6])
        mv_a = sb("mv_a", [P, NT, 2])
        ve_a = sb("ve_a", [P, NT])
        rstd_a = sb("rstd_a", [P, NT])
        qexp = sb("qexp", [P, KT, BS, PAIRS, S])
        kpar = sb("kpar", [P, KT, 2, BT])
        vals = sb("vals", [P, BS, PP, VW])
        probs = sb("probs", [P, 4, H // 2 * S])
        probsT = sb("probsT", [P, 2, H // 2 * S])
        row_max = sb("row_max", [P, 2, H // 2])
        recip = sb("recip", [P, 2, PP, 2])
        attn_n = sb("attn_n", [P, 2, PP, 2, HD])
        attnT = sb("attnT", [P, KT, BT])
        gated_a = sb("gated_a", [P, 2, D])
        pad_u8 = sb("pad_u8", [P, BT], U8)
        pad_bf = sb("pad_bf", [P, BT], BF16)
        gate_m = sb("gate_m", [P, NT, D])
        stats_m = sb("stats_m", [P, NT, 6])
        mv_m = sb("mv_m", [P, NT, 2])
        ve_m = sb("ve_m", [P, NT])
        rstd_m = sb("rstd_m", [P, NT])
        hid = sb("hid", [P, MC, BT])
        gated_m = sb("gated_m", [P, 2, D])
        tmp_mod = sb("tmp_mod", [P, 2, BT])
        wada = hid[:, 0:6, :].rearrange("p a b -> p (a b)").rearrange("p (k n) -> p k n", k=KT)
        wad1 = probsT[:, :, :].rearrange("p k n -> p (k n)").rearrange("p (k n) -> p k n", k=KT)
        wad2 = attnT[:, :, :].rearrange("p k n -> p (k n)").rearrange("p (k n) -> p k n", k=KT)
        stage_wqkv = [[x_in[1][:, :, :].rearrange("p t d -> p (t d)")[:, 0:3 * D], x_attn[1][:, :, :].rearrange("p t d -> p (t d)")[:, 0:3 * D]],
                      [hid[:, 4:7, :].rearrange("p a b -> p (a b)")[:, k * 3 * D:(k + 1) * 3 * D] for k in range(KT)]]
        stage_w1 = [[hid[:, 2 * k:2 * k + 2, :].rearrange("p a b -> p (a b)") for k in range(KT)],
                    [hid[:, 0:2, :].rearrange("p a b -> p (a b)"), x_attn[1][:, :, :].rearrange("p t d -> p (t d)")]]

        def attn_in(l, b):
            return x_in[1 if isinstance(b, int) and b == 1 else l]

        def attn_to(l, b):
            return x_attn[0 if isinstance(b, int) and b == NB - 1 else l]

        def mlp_to(l, b):
            return x_in[1] if l == 0 else attn_to(l, b)

        bank_s = [ctx.enter_context(nc.psum_tensor(f"bank_s{i}", [P, 512], F32)) for i in range(2)]
        bank_t = [ctx.enter_context(nc.psum_tensor(f"bank_t{i}", [P, 512], F32)) for i in range(2)]
        bank_o = [ctx.enter_context(nc.psum_tensor(f"bank_o{i}", [P, 512], F32)) for i in range(2)]
        bank_l = [ctx.enter_context(nc.psum_tensor(f"bank_l{i}", [P, 512], F32)) for i in range(2)]
        q_bank, k_bank = (bank_t[0], bank_s[0]), (bank_t[1], bank_s[1])
        v_at = (bank_o[1][:, 0:D], bank_o[1][:, D:2 * D], bank_t[0][:, 0:D], bank_t[1][:, 0:D])
        gate_dram = nc.dram_tensor("gate_table", [2, NSEQ, D], F32, kind="Internal").ap()

        const_loaded, cond_loaded, cols_loaded = sem("const_loaded"), sem("cond_loaded"), sem("cols_loaded")
        rows_loaded, wada_loaded, wad1_loaded = sem("rows_loaded"), sem("wada_loaded"), sem("wad1_loaded")
        wqkv_loaded, wproj_loaded, w1_loaded, w2_loaded = sems("wqkv_loaded"), sems("wproj_loaded"), sems("w1_loaded"), sems("w2_loaded")
        zeroed, setup_dve, setup_exp = sem("zeroed"), sem("setup_dve"), sem("setup_exp")
        bk_ready, pool_const = sem("bk_ready"), sem("pool_const")
        silu_ready, mods_done, gates_done, fold_done = sem("silu_ready"), sem("mods_done"), sem("gates_done"), sem("fold_done")
        tables_ready, gates_ready = sem("tables_ready"), sem("gates_ready")
        x_loaded, gate_a_loaded, gate_m_loaded = sem("x_loaded"), sem("gate_a_loaded"), sem("gate_m_loaded")
        pad_loaded, pad_ready = sem("pad_loaded"), sem("pad_ready")
        stored = sem("stored")
        stats_done_a, var_done_a, rstd_done_a, xn_done_a = sem("stats_done_a"), sem("var_done_a"), sem("rstd_done_a"), sem("xn_done_a")
        aggr_done_a = sem("aggr_done_a")
        xnT_done_a, mod_mul_a, mod_add_a = sem("xnT_done_a"), sem("mod_mul_a"), sem("mod_add_a")
        hi_done_a, lo_done_a, hi_done_m, lo_done_m = sem("hi_done_a"), sem("lo_done_a"), sem("hi_done_m"), sem("lo_done_m")
        wqkv_hi, wqkv_lo, w1_hi, w1_lo = sems("wqkv_hi"), sems("wqkv_lo"), sems("w1_hi"), sems("w1_lo")
        qk_done, v_done = sem("qk_done"), sem("v_done")
        q_act, q_dve, k_act, k_dve = sem("q_by_act"), sem("q_by_dve"), sem("k_by_act"), sem("k_by_dve")
        v_act, v_dve = sem("v_by_act"), sem("v_by_dve")
        scores_done, max_done, shifted, probs_ready = sem("scores_done"), sem("max_done"), sem("shifted"), sem("probs_ready")
        probsT_done, probsT_ready, pv_done, recip_done = sem("probsT_done"), sem("probsT_ready"), sem("pv_done"), sem("recip_done")
        attn_n_ready, attn_nT_done, attnT_ready = sem("attn_n_ready"), sem("attn_nT_done"), sem("attnT_ready")
        proj_done = sem("proj_done")
        res_a_ready, attn_out = sems("res_a_ready"), sems("attn_out")
        block1_ready = sem("block1_ready")
        proj_gated = sem("proj_gated")
        proj_read = [proj_gated, attn_out[1]]
        bias_a, bias_m = sem("gated_bias_a"), sem("gated_bias_m")
        stats_done_m, aggr_done_m, var_done_m, rstd_done_m, xn_done_m = sem("stats_done_m"), sem("aggr_done_m"), sem("var_done_m"), sem("rstd_done_m"), sem("xn_done_m")
        xnT_done_m, mod_mul_m, mod_add_m = sem("xnT_done_m"), sem("mod_mul_m"), sem("mod_add_m")
        up_done, gelu_done, down_done = sem("up_done"), sem("gelu_done"), sem("down_done")
        res_m_ready, mlp_out = sems("res_m_ready"), sems("mlp_out")
        down_gated = sem("down_gated")
        down_read = [down_gated, mlp_out[1]]

        x_v = a["x"].rearrange("(b t p) d -> b p t d", t=NT, p=P)
        out_v = out.rearrange("(b t p) d -> b p t d", t=NT, p=P)
        gate_v = gate_dram.rearrange("g (b t s) d -> g b s t d", t=NT, s=2)

        def col(name, k=0):
            at = COLS[name][0] + k
            return cols[:, at:at + 1]

        def row(name):
            return rows[:, ROWS.index(name), :]

        block = ctx.enter_context(nc.Block())

        @block.sync
        def _(sp):
            def load_x(b):
                sp.dma_start(attn_in(0, b)[:, :, :], x_v[b]).then_inc(x_loaded, 16)

            def load_gate(which, dst, b, loaded):
                for s in range(2):
                    src = gate_v[which, b, s]
                    sp.dma_start(dst[s * S:(s + 1) * S, :, :], src.unsqueeze(0).to_broadcast([S, NT, D])).then_inc(loaded, 8 * 2)

            def load_pad(at):
                sp.dma_start(pad_u8[:, :], a["pad"][bass.ds(at, BT)].unsqueeze(0).to_broadcast([P, BT])).then_inc(pad_loaded, 16)

            def load_stage(stages, name, loaded):
                for k in range(KT):
                    sp.dma_start(stages[k], a[name][k * P:(k + 1) * P, :]).then_inc(loaded, 16)

            sp.dma_start(condT[:, :, :], a["condT"].rearrange("(k p) n -> p k n", p=P)).then_inc(cond_loaded, 16)
            sp.dma_start(cols[:, :], a["cols"]).then_inc(cols_loaded, 16)
            sp.dma_start(ident[:, :], a["ident"]).then_inc(const_loaded, 16)
            load_x(0)
            sp.dma_start(wada, a["wada"].rearrange("(k p) n -> p k n", p=P)).then_inc(wada_loaded, 16)
            load_stage(stage_wqkv[0], "wqkv0", wqkv_loaded[0])
            sp.dma_start(identb[:, :], a["identb"]).then_inc(const_loaded, 16)
            sp.dma_start(causal[:, :], a["causal"]).then_inc(const_loaded, 16)
            sp.dma_start(rows[:, :, :], a["rows"].unsqueeze(0).to_broadcast([P, len(ROWS), D])).then_inc(rows_loaded, 16)
            sp.dma_start(wad1, a["wad1"].rearrange("(k p) n -> p k n", p=P)).then_inc(wad1_loaded, 16)
            sp.dma_start(wad2, a["wad2"].rearrange("(k p) n -> p k n", p=P)).then_inc(wad1_loaded, 16)
            for l in range(2):
                sp.dma_start(wproj[l][:, :, :], a[f"wproj{l}"].rearrange("(k p) n -> p k n", p=P)).then_inc(wproj_loaded[l], 16)
                sp.dma_start(w2[l][:, :, :], a[f"w2_{l}"].rearrange("(k p) n -> p k n", p=P)).then_inc(w2_loaded[l], 16)
            sp.wait_ge(mods_done, 1)
            sp.wait_ge(gates_done, 1)
            load_stage(stage_w1[0], "w1_0", w1_loaded[0])
            load_stage(stage_wqkv[1], "wqkv1", wqkv_loaded[1])
            sp.wait_ge(gates_ready, 2)
            sp.dma_start(gate_dram.rearrange("g s d -> s g d"), gates[:, :, :]).then_inc(stored, 16)
            sp.wait_ge(stored, 16)
            load_gate(0, gate_a, 0, gate_a_loaded)
            load_gate(1, gate_m, 0, gate_m_loaded)
            sp.wait_ge(wqkv_lo[0], KT)
            load_x(1)
            load_pad(0)
            sp.wait_ge(w1_lo[0], KT)
            load_stage(stage_w1[1], "w1_1", w1_loaded[1])

            def step(st):
                if st.attn:
                    _, l, b = st.attn
                    more = not (isinstance(b, int) and b == NB - 1)
                if st.mlp:
                    _, lm, bm = st.mlp
                    if lm == 1:
                        wait(sp, mlp_out[1], NT * (bm + 1))
                        sp.dma_start(out_v[bm], attn_to(1, bm)[:, :, :]).then_inc(stored, 16)
                if st.attn and l == 0 and more:
                    wait(sp, attn_out[0], NT * (b + 1))
                    if isinstance(b, int) and b == 0:
                        load_x(2)
                    elif not (isinstance(b, int) and b == 1):
                        load_x(b + 1)
                    load_gate(0, gate_a, b + 1, gate_a_loaded)
                if st.attn and l == 1 and more:
                    wait(sp, pad_ready, b + 1)
                if st.mlp and lm == 0 and not (isinstance(bm, int) and bm == NB - 1):
                    wait(sp, down_gated, NT * (bm + 1))
                    load_gate(1, gate_m, bm + 1, gate_m_loaded)
                if st.attn and l == 1 and more:
                    load_pad((b + 1) * BT)

            schedule(sp, step)
            sp.wait_ge(stored, 16 * (NB + 1))

        @block.tensor
        def _(pe):
            seen = set()

            def first_use(sem_, value=16):
                if sem_.name not in seen:
                    seen.add(sem_.name)
                    pe.wait_ge(sem_, value)

            def norm_transposes(n, xn_done, done, banks, free):
                wait(pe, xn_done, NT * (n + 1))
                for k in range(KT):
                    free(k)
                    for t in range(NT):
                        mm = pe.transpose(banks[k][:, t * P:(t + 1) * P], xn[:, t, k * P:(k + 1) * P], ident[:, :])
                    mm.then_inc(done, 1)

            def split_products(out_, lhs, rhs, rest_ready=None):
                terms = ((0, 0), (1, 0), (0, 1))
                passes = [(k, w, x) for w, x in terms[:2] for k in range(KT)] + [(k, *terms[2]) for k in range(KT)]
                for i, (k, w, x) in enumerate(passes):
                    if rest_ready and i == 2 * KT:
                        wait(pe, *rest_ready)
                    mm = pe.matmul(out_, lhs(k, w, x), rhs(k, w, x), start=(i == 0), stop=(i == len(passes) - 1))
                return mm

            def transposes_a(n, after_step=None):
                def free(k):
                    if after_step is not None:
                        wait(pe, shifted, BS * after_step + 7 + k)
                norm_transposes(n, xn_done_a, xnT_done_a, bank_s, free)

            def transposes_m(m):
                def free(k):
                    if m_before[0] is not None:
                        lp, bp = m_before[0]
                        wait(pe, down_read[lp], NT * bp + 3 + k)
                norm_transposes(m, xn_done_m, xnT_done_m, bank_l, free)

            m_before = [None]

            def qkv(n, l, st_mlp):
                first_use(wqkv_hi[l], KT)
                first_use(wqkv_lo[l], KT)
                wait(pe, hi_done_a, KT * (n + 1))
                wait(pe, mod_mul_a, KT * (n + 1))
                for j in range(KT):
                    for c, bank in enumerate((q_bank[j], k_bank[j])):
                        at = c * D + j * P
                        split_products(bank[:, :], lambda k, w, x: wqkv[l][w][:, k, at:at + P], lambda k, w, x: xm[x][:, k, :],
                                       (lo_done_a, KT * (n + 1)) if j == c == 0 else None).then_inc(qk_done, 1)
                if st_mlp:
                    transposes_m(st_mlp[0])
                for t in range(NT):
                    if t == 2:
                        wait(pe, q_act, 6 * n + 3)
                        wait(pe, q_dve, 2 * n + 1)
                    if t == 3:
                        wait(pe, k_act, 2 * n + 2)
                    split_products(v_at[t], lambda k, w, x: xm[x][:, k, t * P:(t + 1) * P], lambda k, w, x: wqkv[l][w][:, k, 2 * D:3 * D]).then_inc(v_done, 1)

            def scores(n, l, b, s):
                if s == 0:
                    if l == 1:
                        wait(pe, pad_ready, b + 1)
                    wait(pe, q_act, 6 * n + 6)
                    wait(pe, q_dve, 2 * n + 2)
                    wait(pe, k_act, 2 * n + 2)
                    wait(pe, k_dve, 2 * n + 2)
                if s >= 2:
                    wait(pe, shifted, BS * n + s - 1)
                bank = bank_s[s % 2]
                mask = causal[:, :] if l == 0 else pad_bf[:, s * S:(s + 1) * S]
                pe.matmul(bank[:, :].rearrange("p (g k) -> p g k", k=S), identb[:, :], mask.unsqueeze(1).to_broadcast([P, H // 2, S]), start=True, stop=False)
                for j in range(KT):
                    for u in range(2):
                        pp = 2 * j + u
                        mm = pe.matmul(bank[:, pp * P:(pp + 1) * P].rearrange("p (e k) -> p e k", e=2), qexp[:, j, s, 2 * u:2 * u + 2, :].rearrange("p a q -> p (a q)"),
                                       kpar[:, j, :, s * S:(s + 1) * S], start=False, stop=(pp == PP - 1))
                mm.then_inc(scores_done, 1)

            def probs_transposes(n, s):
                wait(pe, probs_ready, BS * n + s + 1)
                if s < 2:
                    wait(pe, v_act, 8 * n + 6 + 2 * s)
                    wait(pe, v_dve, 8 * n + 6 + 2 * s)
                else:
                    wait(pe, probsT_ready, BS * n + s - 1)
                for pp in range(PP):
                    mm = pe.transpose(bank_t[s % 2][:, pp * P:(pp + 1) * P], probs[:, s % 4, pp * P:(pp + 1) * P], ident[:, :])
                mm.then_inc(probsT_done, 1)

            def pv(n, l, s, before):
                if isinstance(n, int) and n == 0 and s == 0:
                    pe.wait_ge(gates_ready, 2)
                wait(pe, probsT_ready, BS * n + s + 1)
                wait(pe, attnT_ready, BS * n + s - 1)
                if s % 2 == 0:
                    if s >= 2:
                        wait(pe, proj_read[l], NT * before[2] + s // 2)
                    elif before[0] is not None:
                        wait(pe, proj_read[before[0]], NT * (before[1] + 1))
                for pp in range(PP):
                    mm = pe.matmul(bank_o[s % 2][:, pp * VW:(pp + 1) * VW], probsT[:, s % 2, pp * P:(pp + 1) * P], vals[:, s, pp, :], start=True, stop=True)
                mm.then_inc(pv_done, 1)

            def attn_transpose(n, s):
                wait(pe, attn_n_ready, 16 * n + 2 * s + 2)
                pe.transpose(bank_o[s % 2][:, OT0:OT0 + P], attn_n[:, s % 2, :, :, :].rearrange("p a e d -> p (a e d)"), ident[:, :]).then_inc(attn_nT_done, 1)

            def project(n, l, t):
                first_use(wproj_loaded[l])
                wait(pe, attnT_ready, BS * n + 2 * t + 2)
                for k in range(KT):
                    mm = pe.matmul(bank_o[0][:, 0:D], attnT[:, k, t * P:(t + 1) * P], wproj[l][:, k, :], start=(k == 0), stop=(k == KT - 1))
                mm.then_inc(proj_done, 1)

            def up(m, l, c):
                first_use(w1_hi[l], KT)
                first_use(w1_lo[l], KT)
                if c == 0:
                    wait(pe, hi_done_m, KT * (m + 1))
                    wait(pe, mod_mul_m, KT * (m + 1))
                if c >= 2:
                    wait(pe, gelu_done, MC * m + c - 1)
                split_products(bank_l[c % 2][:, :], lambda k, w, x: w1[l][w][:, k, c * P:(c + 1) * P], lambda k, w, x: xm[x][:, k, :],
                               (lo_done_m, KT * (m + 1)) if c == 0 else None).then_inc(up_done, 1)

            def down(m, l, b, t, first=0, end=MC):
                first_use(w2_loaded[l])
                if first == 0:
                    if t < 2:
                        wait(pe, gelu_done, MC * (m + 1))
                    else:
                        wait(pe, down_read[l], NT * b + t - 1)
                for c in range(first, end):
                    mm = pe.matmul(bank_l[t % 2][:, 0:D], hid[:, c, t * P:(t + 1) * P], w2[l][:, c, :], start=(c == 0), stop=(c == MC - 1))
                if end == MC:
                    mm.then_inc(down_done, 1)

            pe.wait_ge(silu_ready, 1)
            pe.wait_ge(wada_loaded, 16)
            for which, at in enumerate((1, 0, 4, 3)):
                for j in range(KT):
                    for k in range(KT):
                        c0 = at * D + j * P
                        o0 = (which * KT + j) * NSEQ
                        mm = pe.matmul(bank_s[0][:, o0:o0 + NSEQ], wada[:, k, c0:c0 + P], siluT[:, k, :], start=(k == 0), stop=(k == KT - 1))
            mm.then_inc(mods_done, 1)
            for g, at in enumerate((2, 5)):
                for k in range(KT):
                    mm = pe.matmul(bank_o[0][0:NSEQ, g * D:(g + 1) * D], siluT[:, k, :], wada[:, k, at * D:(at + 1) * D], start=(k == 0), stop=(k == KT - 1))
            mm.then_inc(gates_done, 1)
            pe.wait_ge(wad1_loaded, 32)
            for which in range(4):
                w = (wad1, wad2)[which // 2]
                for j in range(KT):
                    for k in range(KT):
                        c0 = (which % 2) * D + j * P
                        o0 = (which * KT + j) * NSEQ
                        mm = pe.matmul(bank_l[0][:, o0:o0 + NSEQ], w[:, k, c0:c0 + P], condT[:, k, :], start=(k == 0), stop=(k == KT - 1))
            mm.then_inc(mods_done, 1)
            pe.wait_ge(const_loaded, 48)
            pe.wait_ge(tables_ready, 1)
            transposes_a(0)

            def step(st):
                m_before[0] = st.before_mlp
                if st.mlp and isinstance(st.mlp[0], int) and st.mlp[0] == 0:
                    pe.wait_ge(tables_ready, 3)
                if st.attn:
                    n, l, b = st.attn
                    before = (*(st.before_attn or (None, None)), b)
                    qkv(n, l, st.mlp)
                if st.mlp:
                    m, lm, bm = st.mlp
                if not st.attn:
                    transposes_m(m)
                    for c in range(MC):
                        up(m, lm, c)
                    for t in range(NT):
                        down(m, lm, bm, t)
                    return
                for s in (0, 1):
                    scores(n, l, b, s)
                if isinstance(n, int) and n == 0:
                    first_use(wproj_loaded[1])
                    for k in range(KT):
                        mm = pe.matmul(bank_l[1][:, 0:D], bv_wide[:, k, :], wproj[1][:, k, :], start=(k == 0), stop=(k == KT - 1))
                    mm.then_inc(fold_done, 1)
                if st.mlp:
                    for c in range(MC // 2):
                        up(m, lm, c)
                for g in range(1, BS // 2):
                    if g != 2:
                        scores(n, l, b, 2 * g)
                    if st.mlp and g == 1:
                        up(m, lm, 4)
                    scores(n, l, b, 2 * g + 1)
                    for s in (2 * g - 2, 2 * g - 1):
                        probs_transposes(n, s)
                    if st.mlp and g == 1:
                        up(m, lm, 5)
                    elif st.mlp:
                        down(m, lm, bm, 0 if g == 2 else 2, 0, MC if g == 2 else 4)
                    for s in (2 * g - 2, 2 * g - 1):
                        pv(n, l, s, before)
                    if g == 1:
                        scores(n, l, b, 4)
                    if st.mlp and g == 1:
                        up(m, lm, 6)
                    elif st.mlp and g == 2:
                        down(m, lm, bm, 1, 0, 4)
                    elif st.mlp:
                        down(m, lm, bm, 2, 4, 6)
                    for s in (2 * g - 2, 2 * g - 1):
                        attn_transpose(n, s)
                    if st.mlp and g == 1:
                        up(m, lm, 7)
                    elif st.mlp and g == 2:
                        down(m, lm, bm, 1, 4, MC)
                    elif st.mlp:
                        down(m, lm, bm, 2, 6, MC)
                    project(n, l, g - 1)
                for s in (6, 7):
                    probs_transposes(n, s)
                if st.nxt and not st.late:
                    transposes_a(st.nxt[0], after_step=n)
                if st.mlp:
                    down(m, lm, bm, 3, 0, 4)
                for s in (6, 7):
                    pv(n, l, s, before)
                if st.mlp:
                    down(m, lm, bm, 3, 4, MC if st.late else 6)
                for s in (6, 7):
                    attn_transpose(n, s)
                if st.mlp and not st.late:
                    down(m, lm, bm, 3, 6, MC)
                project(n, l, 3)
                if st.nxt and st.late:
                    transposes_a(st.nxt[0], after_step=n)

            bv_wide = cols[:, COLS["bv"][0]:COLS["bv"][0] + KT].unsqueeze(2).to_broadcast([P, KT, P])
            pe.wait_ge(cols_loaded, 16)
            pe.wait_ge(zeroed, 3)
            schedule(pe, step)

        @block.vector
        def _(dve):
            def tile_stats(n, x, t, arrived, st_, done, aggr):
                wait(dve, *arrived)
                wait(dve, aggr, NT * n)
                dve.bn_stats(st_[:, t, :], x[:, t, :]).then_inc(done, 1)

            def variances(n, st_, mv, ve, done, aggr, var, read):
                wait(dve, done, NT * (n + 1))
                wait(dve, read, NT * n)
                dve.memset(carrier[:, :], 0.0)
                for t in range(NT):
                    dve.bn_aggr(mv[:, t, :], st_[:, t, :]).then_inc(aggr, 1)
                wait(dve, aggr, NT * (n + 1))
                dve.tensor_scalar(ve[:, :], mv[:, :, 1], EPS, None, ALU.add).then_inc(var, 1)

            def normalise(n, x, mv, rstd, rstd_done, done):
                wait(dve, rstd_done, n + 1)
                for t in range(NT):
                    dve.tensor_scalar(xn[:, t, :], x[:, t, :], mv[:, t, 0:1], rstd[:, t:t + 1], ALU.subtract, ALU.mult).then_inc(done, 1)

            def modulate(n, l, b, norm, banks, xnT_done, mul, add, last=None):
                if last:
                    wait(dve, *last)
                for k in range(KT):
                    wait(dve, xnT_done, KT * n + k + 1)
                    src = banks[k][:, :].rearrange("p (s q) -> p s q", q=S)
                    tmp = tmp_mod[:, k, :].rearrange("p (s q) -> p s q", q=S)
                    factor = mod_mul[:, l, norm, k, bass.ds(BS * b, BS)].unsqueeze(2).to_broadcast([P, BS, S])
                    dve.tensor_tensor(tmp, src, factor, ALU.mult).then_inc(mul, 1)
                for k in range(KT):
                    wait(dve, mul, KT * n + k + 1)
                    tmp = tmp_mod[:, k, :].rearrange("p (s q) -> p s q", q=S)
                    term = mod_add[:, l, norm, k, bass.ds(BS * b, BS)].unsqueeze(2).to_broadcast([P, BS, S])
                    dve.tensor_tensor(tmp, tmp, term, ALU.add).then_inc(add, 1)

            def rest(n, hi, lo):
                for k in range(KT):
                    wait(dve, hi, KT * n + k + 1)
                    dve.tensor_tensor(xm[1][:, k, :], tmp_mod[:, k, :], xm[0][:, k, :].bitcast(F32), ALU.subtract).then_inc(lo, 1)

            def weights_rest(stages, w, hi, lo):
                for k in range(KT):
                    dve.wait_ge(hi, k + 1)
                    dve.tensor_tensor(w[1][:, k, :], stages[k], w[0][:, k, :].bitcast(F32), ALU.subtract).then_inc(lo, 1)

            def tile_stats_a(n, l, b, t):
                arrived = (x_loaded, 16 * (b + 1)) if l == 0 else (mlp_out[0], NT * b + t + 1)
                tile_stats(n, attn_in(l, b), t, arrived, stats_a_buf, stats_done_a, aggr_done_a)

            def variances_a(n):
                variances(n, stats_a_buf, mv_a, ve_a, stats_done_a, aggr_done_a, var_done_a, xn_done_a)

            def stats_a(n, l, b):
                for t in range(NT):
                    tile_stats_a(n, l, b, t)
                variances_a(n)

            def normalise_a(n, l, b, m=-1):
                wait(dve, xnT_done_m, KT * (m + 1))
                normalise(n, attn_in(l, b), mv_a, rstd_a, rstd_done_a, xn_done_a)

            def modulate_a(n, l, b, m=None):
                modulate(n, l, b, 0, bank_s, xnT_done_a, mod_mul_a, mod_add_a, None if m is None else (lo_done_m, KT * (m + 1)))

            def tile_stats_m(m, l, b, t):
                tile_stats(m, attn_to(l, b), t, (attn_out[l], NT * b + t + 1), stats_m, stats_done_m, aggr_done_m)

            def variances_m(m):
                variances(m, stats_m, mv_m, ve_m, stats_done_m, aggr_done_m, var_done_m, xn_done_m)

            def normalise_mlp(m, l, b, n):
                wait(dve, xnT_done_a, KT * (n + 1))
                normalise(m, attn_to(l, b), mv_m, rstd_m, rstd_done_m, xn_done_m)

            def queries(n, l, j):
                wait(dve, qk_done, 4 * n + 2 * j + 1)
                wait(dve, scores_done, BS * n)
                for pr in (3,):
                    r = slice(32 * pr, 32 * pr + 32)
                    dst, src = qexp[r, j, :, pr, :], q_bank[j][r, :].rearrange("p (s q) -> p s q", q=S)
                    if l == 0:
                        i = dve.tensor_copy(dst, src)
                    else:
                        i = dve.tensor_scalar(dst, src, cols[r, COLS["bq"][0] + j:COLS["bq"][0] + j + 1], None, ALU.add)
                    i.then_inc(q_dve, 1)

            def keys(n, l):
                wait(dve, qk_done, 4 * n + 4)
                for e, name in enumerate(("even", "odd")):
                    if l == 0:
                        i = dve.tensor_scalar(kpar[:, 1, e, :], k_bank[1][:, :], col(name), None, ALU.mult)
                    else:
                        i = dve.tensor_scalar(kpar[:, 1, e, :], k_bank[1][:, :], col("bk", 1), col(name), ALU.add, ALU.mult)
                    i.then_inc(k_dve, 1)

            def values(n, t):
                wait(dve, v_done, NT * n + max(t + 1, 2))
                wait(dve, pv_done, BS * n)
                src = v_at[t][S:2 * S, :].rearrange("p (a b e d) -> p a b e d", a=PP, b=2, e=2)
                for e in range(2):
                    dst = vals[e * S:(e + 1) * S, 2 * t + 1, :, 0:4 * HD].rearrange("p a (b e d) -> p a b e d", b=2, e=2)
                    dve.tensor_copy(dst[:, :, :, e, :], src[:, :, :, e, :]).then_inc(v_dve, 1)

            def pad_mask(n, b):
                wait(dve, pad_loaded, 16 * (b + 1))
                wait(dve, scores_done, BS * n)
                dve.tensor_scalar(pad_bf[:, :], pad_u8[:, :], MASKED, None, ALU.mult).then_inc(pad_ready, 1)

            def shift(n, s):
                bank = bank_s[s % 2][:, :].rearrange("p (g k) -> p g k", k=S)
                wait(dve, scores_done, BS * n + s + 1)
                dve.tensor_reduce(row_max[:, s % 2, :], bank, AX.X, ALU.max).then_inc(max_done, 1)
                wait(dve, max_done, BS * n + s + 1)
                wait(dve, probsT_done, BS * n + s - 3)
                dve.tensor_tensor(probs[:, s % 4, :].rearrange("p (g k) -> p g k", k=S), bank, row_max[:, s % 2, :].unsqueeze(2).to_broadcast([P, H // 2, S]),
                                  ALU.subtract).then_inc(shifted, 1)

            def divide(n, s):
                bank = bank_o[s % 2][:, 0:PP * VW].rearrange("p (a w) -> p a w", a=PP)
                wait(dve, pv_done, BS * n + s + 1)
                dve.reciprocal(recip[:, s % 2, :, :], bank[:, :, 4 * HD:4 * HD + 2]).then_inc(recip_done, 1)
                wait(dve, recip_done, BS * n + s + 1)
                wait(dve, attn_nT_done, BS * n + s - 1)
                for b in range(2):
                    r = slice(b * S, (b + 1) * S)
                    src = bank[r, :, b * 2 * HD:(b + 1) * 2 * HD].rearrange("p a (e d) -> p a e d", e=2)
                    dve.tensor_tensor(attn_n[r, s % 2, :, :, :], src, recip[r, s % 2, :, :].unsqueeze(3).to_broadcast([S, PP, 2, HD]), ALU.mult).then_inc(attn_n_ready, 1)

            def add_projection(n, l, b, t):
                wait(dve, proj_done, NT * n + t + 1)
                if l == 0:
                    wait(dve, gate_a_loaded, 32 * (b + 1))
                    dve.tensor_tensor(gated_a[:, t % 2, :], bank_o[0][:, 0:D], gate_a[:, t, :], ALU.mult).then_inc(proj_gated, 1)
                    wait(dve, proj_gated, NT * b + t + 1)
                    src = gated_a[:, t % 2, :]
                else:
                    src = bank_o[0][:, 0:D]
                wait(dve, res_a_ready[l], NT * b + t + 1)
                if isinstance(n, int) and n == 1:
                    dve.tensor_tensor(src, src, attn_in(l, b)[:, t, :], ALU.add).then_inc(block1_ready, 1)
                    return
                if l == 0:
                    wait(dve, mlp_out[0], NT * b)
                elif isinstance(b, int) and b == NB - 1:
                    dve.wait_ge(mlp_out[0], NT * NB)
                else:
                    wait(dve, stored, 16 * (b + 1))
                dve.tensor_tensor(attn_to(l, b)[:, t, :], src, attn_in(l, b)[:, t, :], ALU.add).then_inc(attn_out[l], 1)

            def take_place(t):
                dve.wait_ge(block1_ready, t + 1)
                dve.wait_ge(mlp_out[0], t + 1)
                dve.tensor_copy(x_attn[0][:, t, :], gated_a[:, t % 2, :]).then_inc(attn_out[0], 1)

            def add_down(m, l, b, t):
                wait(dve, down_done, NT * m + t + 1)
                if l == 0:
                    wait(dve, gate_m_loaded, 32 * (b + 1))
                    dve.tensor_tensor(gated_m[:, t % 2, :], bank_l[t % 2][:, 0:D], gate_m[:, t, :], ALU.mult).then_inc(down_gated, 1)
                    wait(dve, down_gated, NT * b + t + 1)
                    src = gated_m[:, t % 2, :]
                    if isinstance(b, int) and b == 0:
                        dve.wait_ge(block1_ready, t + 1)
                    else:
                        wait(dve, attn_out[1], NT * (b - 1) + t + 1)
                else:
                    src = bank_l[t % 2][:, 0:D]
                wait(dve, res_m_ready[l], NT * b + t + 1)
                dve.tensor_tensor(mlp_to(l, b)[:, t, :], src, attn_to(l, b)[:, t, :], ALU.add).then_inc(mlp_out[l], 1)

            dve.memset(qexp[:, :, :, :, :], 0.0).then_inc(zeroed, 1)
            dve.memset(vals[:, :, :, :], 0.0).then_inc(zeroed, 1)
            dve.wait_ge(setup_exp, 1)
            dve.tensor_scalar(siluT[:, :, :], siluT[:, :, :], 1.0, None, ALU.add).then_inc(setup_dve, 1)
            dve.wait_ge(setup_dve, 1)
            dve.reciprocal(siluT[:, :, :], siluT[:, :, :]).then_inc(setup_dve, 1)
            dve.wait_ge(setup_dve, 2)
            dve.tensor_tensor(siluT[:, :, :], siluT[:, :, :], condT[:, :, :], ALU.mult).then_inc(silu_ready, 1)
            dve.wait_ge(zeroed, 2)
            for e in range(2):
                i = dve.memset(vals[e * S:(e + 1) * S, :, :, 4 * HD + e:4 * HD + e + 1], 1.0)
            i.then_inc(zeroed, 1)
            stats_a(0, 0, 0)
            normalise_a(0, 0, 0)
            dve.wait_ge(cols_loaded, 16)
            for i, name in enumerate(("bada_sc_a", "bada_sc_m", "sc1_1", "sc2_1")):
                at = COLS[name][0]
                dve.tensor_scalar(col1[:, 2 * i:2 * i + 2], cols[:, at:at + 2], 1.0, None, ALU.add).then_inc(setup_dve, 1)
            dve.wait_ge(setup_dve, 6)
            dve.wait_ge(mods_done, 1)
            n_tab = 6
            for norm, (g, be, sh) in enumerate((("g1", "be1", "bada_sh_a"), ("g2", "be2", "bada_sh_m"))):
                for k in range(KT):
                    sc_ps = bank_s[0][:, (2 * norm * KT + k) * NSEQ:(2 * norm * KT + k + 1) * NSEQ]
                    sh_ps = bank_s[0][:, ((2 * norm + 1) * KT + k) * NSEQ:((2 * norm + 1) * KT + k + 1) * NSEQ]
                    one = col1[:, 2 * norm + k:2 * norm + k + 1]
                    dve.tensor_scalar(mod_mul[:, 0, norm, k, :], sc_ps, one, col(g, k), ALU.add, ALU.mult).then_inc(setup_dve, 1)
                    dve.tensor_scalar(tmp_mod[:, k, norm * NSEQ:(norm + 1) * NSEQ], sc_ps, one, col(be, k), ALU.add, ALU.mult).then_inc(setup_dve, 1)
                    n_tab += 2
                    dve.wait_ge(setup_dve, n_tab)
                    i = dve.scalar_tensor_tensor(out=mod_add[:, 0, norm, k, :], in0=sh_ps, scalar=col(sh, k), in1=tmp_mod[:, k, norm * NSEQ:(norm + 1) * NSEQ],
                                                 op0=ALU.add, op1=ALU.add)
            i.then_inc(tables_ready, 1)
            dve.wait_ge(tables_ready, 1)
            modulate_a(0, 0, 0)
            weights_rest(stage_wqkv[0], wqkv[0], wqkv_hi[0], wqkv_lo[0])
            rest(0, hi_done_a, lo_done_a)
            dve.wait_ge(gates_done, 1)
            dve.wait_ge(rows_loaded, 16)
            for g, name in enumerate(("bada_gt_a", "bada_gt_m")):
                dve.tensor_tensor(gates[:, g, :], bank_o[0][0:NSEQ, g * D:(g + 1) * D], rows[0:NSEQ, ROWS.index(name), :], ALU.add).then_inc(gates_ready, 1)
            dve.wait_ge(mods_done, 2)
            for norm, sh in enumerate(("sh1_1", "sh2_1")):
                for k in range(KT):
                    sc_ps = bank_l[0][:, (2 * norm * KT + k) * NSEQ:(2 * norm * KT + k + 1) * NSEQ]
                    sh_ps = bank_l[0][:, ((2 * norm + 1) * KT + k) * NSEQ:((2 * norm + 1) * KT + k + 1) * NSEQ]
                    dve.tensor_scalar(mod_mul[:, 1, norm, k, :], sc_ps, col1[:, 4 + 2 * norm + k:5 + 2 * norm + k], None, ALU.add)
                    i = dve.tensor_scalar(mod_add[:, 1, norm, k, :], sh_ps, col(sh, k), None, ALU.add)
            i.then_inc(tables_ready, 1)
            dve.wait_ge(tables_ready, 2)

            def step(st):
                m = None
                if st.mlp:
                    m, lm, bm = st.mlp
                if not st.attn:
                    normalise_mlp(m, lm, bm, m)
                    modulate(m, lm, bm, 1, bank_l, xnT_done_m, mod_mul_m, mod_add_m)
                    rest(m, hi_done_m, lo_done_m)
                    for t in range(NT):
                        add_down(m, lm, bm, t)
                    return
                n, l, b = st.attn
                queries(n, l, 0)
                if st.mlp:
                    normalise_mlp(m, lm, bm, n)
                queries(n, l, 1)
                keys(n, l)
                if st.mlp:
                    modulate(m, lm, bm, 1, bank_l, xnT_done_m, mod_mul_m, mod_add_m, (lo_done_a, KT * (n + 1)))
                for t in range(NT):
                    if st.mlp and t == 2:
                        rest(m, hi_done_m, lo_done_m)
                    values(n, t)
                shift(n, 0)
                shift(n, 1)
                if isinstance(n, int) and n == 0:
                    dve.wait_ge(fold_done, 1)
                    dve.tensor_tensor(row("bproj_1"), bank_l[1][:, 0:D], row("bproj_1"), ALU.add).then_inc(tables_ready, 1)

                def add_tiles(t):
                    both_first = st.mlp and lm == l == 0
                    add_projection(n, l, b, t)
                    if not both_first:
                        tile_stats_m(n, l, b, t)
                    if st.mlp and t > 0:
                        add_down(m, lm, bm, t)
                        if st.late:
                            tile_stats_a(*st.nxt, t)
                        if both_first:
                            take_place(t)
                            tile_stats_m(n, l, b, t)

                for g in range(1, BS // 2):
                    shift(n, 2 * g)
                    shift(n, 2 * g + 1)
                    if g == 2 and st.nxt and not st.late:
                        stats_a(*st.nxt)
                    if g == 3 and st.nxt and st.nxt[1] == 1:
                        pad_mask(st.nxt[0], st.nxt[2])
                    if g == 3 and st.nxt and not st.late:
                        normalise_a(*st.nxt, m if st.mlp else -1)
                    if st.mlp and g == 2:
                        add_down(m, lm, bm, 0)
                        if st.late:
                            tile_stats_a(*st.nxt, 0)
                        if lm == l == 0:
                            take_place(0)
                            tile_stats_m(n, l, b, 0)
                    divide(n, 2 * g - 2)
                    divide(n, 2 * g - 1)
                    add_tiles(g - 1)
                if st.nxt and not st.late:
                    modulate_a(*st.nxt, m)
                divide(n, 6)
                divide(n, 7)
                if st.nxt and not st.late:
                    rest(st.nxt[0], hi_done_a, lo_done_a)
                add_tiles(3)
                if st.late:
                    variances_a(st.nxt[0])
                variances_m(n)
                if st.late:
                    normalise_a(*st.nxt, m)
                    modulate_a(*st.nxt, m)
                    rest(st.nxt[0], hi_done_a, lo_done_a)

            schedule(dve, step)

        @block.scalar
        def _(act):
            def queries(n, l, j):
                wait(act, qk_done, 4 * n + 2 * j + 1)
                wait(act, scores_done, BS * n)
                for pr in (0, 1, 2):
                    r = slice(32 * pr, 32 * pr + 32)
                    bias = 0.0 if l == 0 else cols[r, COLS["bq"][0] + j:COLS["bq"][0] + j + 1]
                    act.activation(qexp[r, j, :, pr, :], q_bank[j][r, :].rearrange("p (s q) -> p s q", q=S), ACT.Identity, bias=bias).then_inc(q_act, 1)

            def keys(n, l):
                wait(act, qk_done, 4 * n + 2)
                for e, name in enumerate(("even", "odd")):
                    bias = 0.0 if l == 0 else bk_par[:, e:e + 1]
                    act.activation(kpar[:, 0, e, :], k_bank[0][:, :], ACT.Identity, bias=bias, scale=col(name)).then_inc(k_act, 1)

            def values(n, t):
                wait(act, v_done, NT * n + max(t + 1, 2))
                wait(act, pv_done, BS * n)
                src = v_at[t][0:S, :].rearrange("p (a b e d) -> p a b e d", a=PP, b=2, e=2)
                for e in range(2):
                    dst = vals[e * S:(e + 1) * S, 2 * t, :, 0:4 * HD].rearrange("p a (b e d) -> p a b e d", b=2, e=2)
                    act.activation(dst[:, :, :, e, :], src[:, :, :, e, :], ACT.Copy).then_inc(v_act, 1)

            def exps(n, s):
                wait(act, shifted, BS * n + s + 1)
                act.activation(probs[:, s % 4, :], probs[:, s % 4, :], ACT.Exp, scale=SCALE).then_inc(probs_ready, 1)

            def read_probsT(n, s):
                wait(act, probsT_done, BS * n + s + 1)
                wait(act, pv_done, BS * n + s - 1)
                act.activation(probsT[:, s % 2, :], bank_t[s % 2][:, :], ACT.Copy).then_inc(probsT_ready, 1)

            def read_attnT(n, s):
                wait(act, attn_nT_done, BS * n + s + 1)
                if s == 0:
                    wait(act, proj_done, NT * n)
                act.activation(attnT[:, :, s * S:(s + 1) * S], bank_o[s % 2][:, OT0:OT0 + P].rearrange("p (k q) -> p k q", k=KT), ACT.Copy).then_inc(attnT_ready, 1)

            def load_gelu():
                act.wait_ge(pool_const, 1)
                act.activation(gelu_carrier[:, :], half_neg[:, 0:1], ACT.Gelu)

            def gelu(m, l, c):
                wait(act, up_done, MC * m + c + 1)
                if c == 0 and isinstance(m, int) and m == 0:
                    act.wait_ge(w1_lo[0], KT)
                    act.wait_ge(wqkv_lo[1], KT)
                    act.wait_ge(w1_lo[1], KT)
                elif c == 0:
                    wait(act, down_done, NT * m)
                act.activation(hid[:, c, :], bank_l[c % 2][:, :], ACT.Gelu, bias=col(f"b1_{l}", c)).then_inc(gelu_done, 1)

            def modulated_hi(n, add, hi, read=None):
                if read:
                    wait(act, *read)
                for k in range(KT):
                    wait(act, add, KT * n + k + 1)
                    act.activation(xm[0][:, k, :], tmp_mod[:, k, :], ACT.Copy).then_inc(hi, 1)

            def weights_hi(stages, w, loaded, hi):
                act.wait_ge(loaded, 16 * KT)
                for k in range(KT):
                    act.activation(w[0][:, k, :], stages[k], ACT.Copy).then_inc(hi, 1)

            act.wait_ge(cond_loaded, 16)
            act.activation(siluT[:, :, :], condT[:, :, :], ACT.Exp, scale=-1.0).then_inc(setup_exp, 1)
            act.wait_ge(cols_loaded, 16)
            for e, name in enumerate(("even", "odd")):
                act.activation(bk_par[:, e:e + 1], col("bk"), ACT.Identity, scale=col(name)).then_inc(bk_ready, 1)
            weights_hi(stage_wqkv[0], wqkv[0], wqkv_loaded[0], wqkv_hi[0])
            modulated_hi(0, mod_add_a, hi_done_a)
            act.wait_ge(bk_ready, 2)
            act.wait_ge(zeroed, 3)

            def step(st):
                if st.mlp:
                    m, lm, bm = st.mlp
                if not st.attn:
                    load_gelu()
                    modulated_hi(m, mod_add_m, hi_done_m)
                    for c in range(MC):
                        gelu(m, lm, c)
                    return
                n, l, b = st.attn
                queries(n, l, 0)
                keys(n, l)
                queries(n, l, 1)
                for t in range(NT):
                    values(n, t)
                if st.mlp:
                    modulated_hi(m, mod_add_m, hi_done_m, (v_done, NT * (n + 1)))
                    load_gelu()
                    for c in range(MC // 2):
                        gelu(m, lm, c)
                exps(n, 0)
                exps(n, 1)
                for g in range(1, BS // 2):
                    read_probsT(n, 2 * g - 2)
                    read_probsT(n, 2 * g - 1)
                    exps(n, 2 * g)
                    exps(n, 2 * g + 1)
                    if isinstance(n, int) and n == 0 and g == 1:
                        weights_hi(stage_w1[0], w1[0], w1_loaded[0], w1_hi[0])
                    if isinstance(n, int) and n == 0 and g == 2:
                        weights_hi(stage_wqkv[1], wqkv[1], wqkv_loaded[1], wqkv_hi[1])
                    if st.mlp and g == 1:
                        for c in (4, 5, 6):
                            gelu(m, lm, c)
                    read_attnT(n, 2 * g - 2)
                    read_attnT(n, 2 * g - 1)
                    if st.mlp and g == 1:
                        gelu(m, lm, 7)
                read_probsT(n, 6)
                read_probsT(n, 7)
                if st.nxt and not st.late:
                    modulated_hi(st.nxt[0], mod_add_a, hi_done_a)
                read_attnT(n, 6)
                read_attnT(n, 7)
                if isinstance(n, int) and n == 0:
                    weights_hi(stage_w1[1], w1[1], w1_loaded[1], w1_hi[1])
                if st.late:
                    modulated_hi(st.nxt[0], mod_add_a, hi_done_a)

            schedule(act, step)

        @block.gpsimd
        def _(pool):
            def rstd(n, ve, out_, var, xn_done, done):
                wait(pool, var, n + 1)
                wait(pool, xn_done, NT * n)
                pool.tensor_tensor(out_[:, :], ve[:, :], half_neg[:, :], ALU.pow).then_inc(done, 1)

            def residual(l, b, kind, xn_done, count):
                x, gate, loaded, ready, gated, bias = ((attn_in(l, b), gate_a, gate_a_loaded, res_a_ready, bias_a, row(f"bproj_{l}")) if kind == "a" else
                                                       (attn_to(l, b), gate_m, gate_m_loaded, res_m_ready, bias_m, row(f"b2_{l}")))
                if l == 0:
                    wait(pool, loaded, 32 * (b + 1))
                wait(pool, xn_done, count)
                for t in range(NT):
                    if l == 0:
                        pool.tensor_tensor(gate_bias[:, t % 2, :], gate[:, t, :], bias, ALU.mult).then_inc(gated, 1)
                        wait(pool, gated, NT * b + t + 1)
                    pool.tensor_tensor(x[:, t, :], x[:, t, :], gate_bias[:, t % 2, :] if l == 0 else bias, ALU.add).then_inc(ready[l], 1)

            pool.memset(half_neg[:, :], -0.5).then_inc(pool_const, 1)
            pool.wait_ge(pool_const, 1)
            rstd(0, ve_a, rstd_a, var_done_a, xn_done_a, rstd_done_a)
            pool.wait_ge(rows_loaded, 16)

            def weights_rest(stages, w, hi, lo):
                for k in range(KT):
                    pool.wait_ge(hi, k + 1)
                    pool.tensor_tensor(w[1][:, k, :], stages[k], w[0][:, k, :].bitcast(F32), ALU.subtract).then_inc(lo, 1)

            def step(st):
                if st.mlp:
                    m, lm, bm = st.mlp
                if st.attn:
                    if isinstance(st.attn[0], int) and st.attn[0] == 2:
                        pool.wait_ge(tables_ready, 3)
                    residual(st.attn[1], st.attn[2], "a", xn_done_a, NT * (st.attn[0] + 1))
                if st.mlp:
                    residual(lm, bm, "m", xn_done_m, NT * (m + 1))
                first = st.attn and isinstance(st.attn[0], int) and st.attn[0] == 0
                if st.nxt:
                    rstd(st.nxt[0], ve_a, rstd_a, var_done_a, xn_done_a, rstd_done_a)
                if first:
                    weights_rest(stage_w1[0], w1[0], w1_hi[0], w1_lo[0])
                    weights_rest(stage_wqkv[1], wqkv[1], wqkv_hi[1], wqkv_lo[1])
                    weights_rest(stage_w1[1], w1[1], w1_hi[1], w1_lo[1])
                if st.attn:
                    rstd(st.attn[0], ve_m, rstd_m, var_done_m, xn_done_m, rstd_done_m)

            schedule(pool, step)


def layer_columns(v):
    return np.asarray(v).reshape(-1, P).T


def by_pair_parity(w):
    w = np.asarray(w)
    return w.reshape(PP, 2, 2 * HD, -1).transpose(1, 0, 2, 3).reshape(w.shape)


def kernel(**inputs):
    import concourse.bacc as bacc
    from concourse.bass_utils import run_bass_kernel_spmd

    v = {k: np.asarray(x) for k, x in inputs.items()}
    L0 = {k[8:]: x for k, x in v.items() if k.startswith("L0_cond_")}
    L1 = {k[8:]: x for k, x in v.items() if k.startswith("L1_cond_")}
    f32 = np.float32
    even = (np.arange(P) // HD % 2 == 0).astype(f32)
    bada, ad1, ad2 = L0["bada"].reshape(6, D), L1["b_adaln1"].reshape(2, D), L1["b_adaln2"].reshape(2, D)
    vectors = {
        "g1": L0["g1"], "be1": L0["be1"], "g2": L0["g2"], "be2": L0["be2"],
        "bada_sc_a": bada[1], "bada_sh_a": bada[0], "bada_sc_m": bada[4], "bada_sh_m": bada[3], "b1_0": L0["b1"],
        "sc1_1": ad1[0], "sh1_1": ad1[1], "sc2_1": ad2[0], "sh2_1": ad2[1],
        "bq": L1["bq"], "bk": L1["bk"], "bv": by_pair_parity(L1["bv"]), "b1_1": L1["b1"],
        "even": even, "odd": np.where(even > 0, f32(0), f32(1)),
    }
    bf16 = mybir.dt.np(BF16)
    q, k = np.arange(P)[:, None] % S, np.arange(S)[None, :]
    arrays = {
        "x": v["x"].reshape(NSEQ * S, D),
        "pad": v["mask_BxS_bf0"].reshape(-1),
        "condT": v["cond_1024"].T,
        "cols": np.concatenate([layer_columns(vectors[name]) for name in COLS], axis=1),
        "rows": np.stack([L0["bproj"], L1["bo"], L0["b2"], L1["b2"], bada[2], bada[5]]),
        "ident": np.eye(P, dtype=f32),
        "identb": np.eye(P, dtype=f32).astype(bf16),
        "causal": np.where(k <= q, 0.0, MASKED).astype(bf16),
        "wada": L0["Wada"],
        "wad1": L1["w_adaln1"].T, "wad2": L1["w_adaln2"].T,
        "wqkv0": L0["Wqkv"], "wqkv1": np.concatenate([L1["wq"].T, L1["wk"].T, L1["wv"].T], axis=1),
        "wproj0": by_pair_parity(L0["Wproj"]), "wproj1": by_pair_parity(L1["wo"].T),
        "w1_0": L0["W1"], "w1_1": L1["w1"].T,
        "w2_0": L0["W2"], "w2_1": L1["w2"].T,
    }
    arrays = {k_: np.ascontiguousarray(x) for k_, x in arrays.items()}
    nc = bacc.Bacc("TRN2", target_bir_lowering=False, num_devices=1)
    aps = {k_: nc.dram_tensor(f"in_{k_}", x.shape, mybir.dt.from_np(x.dtype), kind="ExternalInput").ap() for k_, x in arrays.items()}
    out = nc.dram_tensor("out", (NSEQ * S, D), F32, kind="ExternalOutput").ap()
    build(nc, aps, out)
    r = run_bass_kernel_spmd(nc, [{f"in_{k_}": x for k_, x in arrays.items()}], core_ids=[0])
    return r.results[0]["out"].reshape(NSEQ, S, D)
```

```python
from contextlib import ExitStack

import numpy as np

import concourse.bass as bass
from concourse import mybir

F32 = mybir.dt.float32
F32R = mybir.dt.float32r
BF16 = mybir.dt.bfloat16
U8 = mybir.dt.uint8
ALU = mybir.AluOpType
ACT = mybir.ActivationFunctionType
AX = mybir.AxisListType

P = 128
NSEQ, S, D = 64, 64, 256
H, HD = 16, 16
MLP = 1024
BS = 8
NB = NSEQ // BS
BT = BS * S
NT = BT // P
KT = D // P
MC = MLP // P
PAIRS = P // (2 * HD)
PP = H // 4
VW = 4 * HD + 2
OT0 = 384
PARTS = (range(0, NT - 1), range(NT - 1, NT))
EPS = 1e-5
MASKED = -1e30
SCALE = HD ** -0.5

COLS = {}
for _name, _n in (("g1", 2), ("be1", 2), ("g2", 2), ("be2", 2), ("bada_sc_a", 2), ("bada_sh_a", 2),
                  ("bada_sc_m", 2), ("bada_sh_m", 2), ("b1_0", 8), ("sc1_1", 2), ("sh1_1", 2),
                  ("sc2_1", 2), ("sh2_1", 2), ("bq", 2), ("bk", 2), ("bv", 2), ("b1_1", 8),
                  ("even", 1), ("odd", 1)):
    COLS[_name] = (sum(n for _, n in COLS.values()), _n)
NCOLS = sum(n for _, n in COLS.values())
ROWS = ("bproj_0", "bproj_1", "b2_0", "b2_1")


class Step:

    def __init__(self, attn, mlp, nxt, before_attn=None, before_mlp=None, late=False):
        self.attn, self.mlp, self.nxt = attn, mlp, nxt
        self.before_attn, self.before_mlp, self.late = before_attn, before_mlp, late


def even_step(i):
    return Step((2 * i - 1, 0, i), (2 * i - 2, 1, i - 2), (2 * i, 1, i - 1), (1, i - 2), (0, i - 1))


def odd_step(i, last=False):
    nxt = (2 * i + 1, 1, i) if last else (2 * i + 1, 0, i + 1)
    return Step((2 * i, 1, i - 1), (2 * i - 1, 0, i), nxt, (0, i), (1, i - 2), late=last)


def schedule(eng, step):
    step(Step((0, 0, 0), None, (1, 0, 1)))
    step(Step((1, 0, 1), (0, 0, 0), (2, 1, 0), (0, 0), None, late=True))
    step(Step((2, 1, 0), (1, 0, 1), (3, 0, 2), (0, 1), (0, 0)))
    with eng.Fori(2, NB - 1) as i:
        step(even_step(i))
        step(odd_step(i))
    step(even_step(NB - 1))
    step(odd_step(NB - 1, last=True))
    step(Step((2 * NB - 1, 1, NB - 1), (2 * NB - 2, 1, NB - 2), None, (1, NB - 2), (0, NB - 1)))
    step(Step(None, (2 * NB - 1, 1, NB - 1), None, (1, NB - 1), (1, NB - 2)))


def wait(eng, sem, value):
    if isinstance(value, int) and value <= 0:
        return
    eng.wait_ge(sem, value)


def build(nc, a, out):
    with ExitStack() as ctx:
        def sb(name, shape, dt=F32):
            return ctx.enter_context(nc.sbuf_tensor(name, shape, dt))

        def sem(name):
            return ctx.enter_context(nc.semaphore(name))

        def sems(name):
            return [sem(f"{name}_l0"), sem(f"{name}_l1")]

        ident = sb("ident", [P, P])
        causal = sb("causal", [P, S], BF16)
        cols = sb("cols", [P, NCOLS])
        rows = sb("rows", [P, len(ROWS), D])
        wqkv = [[sb(f"wqkv{l}_{part}", [P, KT, 3 * D], F32R) for part in ("hi", "lo")] for l in range(2)]
        wproj = [[sb(f"wproj{l}_{part}", [P, KT, D], F32R) for part in ("hi", "lo")] for l in range(2)]
        w1 = [[sb(f"w1_{l}_{part}", [P, KT, MLP], F32R) for part in ("hi", "lo")] for l in range(2)]
        w2 = [sb(f"w2_{l}", [P, MC, D]) for l in range(2)]
        mod_mul = sb("mod_mul", [P, 2, 2, KT, NSEQ])
        mod_add = sb("mod_add", [P, 2, 2, KT, NSEQ])
        carrier = sb("carrier", [P, 1])
        gelu_carrier = sb("gelu_carrier", [P, 1])
        bk_par = sb("bk_par", [P, 2])
        half_neg = sb("half_neg", [P, NT])
        condT = sb("condT", [P, KT, NSEQ])
        siluT = sb("siluT", [P, KT, NSEQ])
        table_tmp = sb("table_tmp", [P, KT, NSEQ])
        col1 = sb("col1", [P, 8])
        x_in = [sb("x_in", [P, NT, D]), sb("x_mid", [P, NT, D])]
        x_attn = [sb(f"x_attn{l}", [P, NT, D]) for l in range(2)]
        xn = sb("xn", [P, NT, D])
        xm = [sb(f"xm_{part}", [P, KT, BT], F32R) for part in ("hi", "lo")]
        gate_bias = sb("gate_bias", [P, 2, D])
        gate_a = sb("gate_a", [P, NT, D])
        stats_a_buf = sb("stats_a", [P, NT, 6])
        mv_a = sb("mv_a", [P, NT, 2])
        ve_a = sb("ve_a", [P, NT])
        rstd_a = sb("rstd_a", [P, NT])
        qexp = sb("qexp", [P, KT, BS, PAIRS, S])
        kpar = sb("kpar", [P, KT, 2, BT])
        vals = sb("vals", [P, BS, PP, VW])
        probs = sb("probs", [P, 4, H // 2 * S])
        probsT = sb("probsT", [P, 2, H // 2 * S])
        row_max = sb("row_max", [P, 2, H // 2])
        recip = sb("recip", [P, 2, PP, 2])
        attn_n = sb("attn_n", [P, 2, PP, 2, HD])
        attnT = [sb(f"attnT_{part}", [P, KT, BT], F32R) for part in ("hi", "lo")]
        gated_a = sb("gated_a", [P, 2, D])
        pad_u8 = sb("pad_u8", [P, BT], U8)
        pad_bf = sb("pad_bf", [P, BT], BF16)
        gate_m = sb("gate_m", [P, NT, D])
        stats_m = sb("stats_m", [P, NT, 6])
        mv_m = sb("mv_m", [P, NT, 2])
        ve_m = sb("ve_m", [P, NT])
        rstd_m = sb("rstd_m", [P, NT])
        hid = sb("hid", [P, MC, BT])
        gated_m = sb("gated_m", [P, 2, D])
        tmp_mod = sb("tmp_mod", [P, 2, BT])
        wada = hid[:, 0:6, :].rearrange("p a b -> p (a b)").rearrange("p (k n) -> p k n", k=KT)
        wad1 = probsT[:, :, :].rearrange("p k n -> p (k n)").rearrange("p (k n) -> p k n", k=KT)
        wad2 = x_attn[0][:, :, :].rearrange("p t d -> p (t d)").rearrange("p (k n) -> p k n", k=KT)
        bada_gates, gates = gated_a[0:NSEQ, :, :], gated_m[0:NSEQ, :, :]
        stage_wqkv = [[x_in[1][:, :, :].rearrange("p t d -> p (t d)")[:, 0:3 * D], x_attn[1][:, :, :].rearrange("p t d -> p (t d)")[:, 0:3 * D]],
                      [hid[:, 4:7, :].rearrange("p a b -> p (a b)")[:, k * 3 * D:(k + 1) * 3 * D] for k in range(KT)]]
        stage_wproj = [[hid[:, 7, k * D:(k + 1) * D] for k in range(KT)],
                       [x[:, NT - 1, :] for x in (x_in[1], x_attn[1])]]
        stage_w1 = [[hid[:, 2 * k:2 * k + 2, :].rearrange("p a b -> p (a b)") for k in range(KT)],
                    [hid[:, 0:2, :].rearrange("p a b -> p (a b)"), x_attn[1][:, :, :].rearrange("p t d -> p (t d)")]]

        def attn_in(l, b):
            return x_in[1 if isinstance(b, int) and b == 1 else l]

        def attn_to(l, b):
            return x_attn[0 if isinstance(b, int) and b == NB - 1 else l]

        def mlp_to(l, b):
            return x_in[1] if l == 0 else attn_to(l, b)

        bank_s = [ctx.enter_context(nc.psum_tensor(f"bank_s{i}", [P, 512], F32)) for i in range(2)]
        bank_t = [ctx.enter_context(nc.psum_tensor(f"bank_t{i}", [P, 512], F32)) for i in range(2)]
        bank_o = [ctx.enter_context(nc.psum_tensor(f"bank_o{i}", [P, 512], F32)) for i in range(2)]
        bank_l = [ctx.enter_context(nc.psum_tensor(f"bank_l{i}", [P, 512], F32)) for i in range(2)]
        q_bank, k_bank = (bank_t[0], bank_s[0]), (bank_t[1], bank_s[1])
        v_at = (bank_o[1][:, 0:D], bank_o[1][:, D:2 * D], bank_t[0][:, 0:D], bank_t[1][:, 0:D])
        gate_dram = nc.dram_tensor("gate_table", [2, NSEQ, D], F32, kind="Internal").ap()

        ident_loaded, const_loaded, cond_loaded, cols_loaded = sem("ident_loaded"), sem("const_loaded"), sem("cond_loaded"), sem("cols_loaded")
        bada_loaded = sem("bada_loaded")
        rows_loaded, wada_a_loaded, wada_loaded, wad1_loaded = sem("rows_loaded"), sem("wada_a_loaded"), sem("wada_loaded"), sem("wad1_loaded")
        wqkv_loaded, wproj_loaded, w1_loaded, w2_loaded = sems("wqkv_loaded"), sems("wproj_loaded"), sems("w1_loaded"), sems("w2_loaded")
        zeroed, setup_dve, setup_exp = sem("zeroed"), sem("setup_dve"), sem("setup_exp")
        bk_ready, pool_const = sem("bk_ready"), sem("pool_const")
        silu_ready, mods_done, gates_done, fold_done = sem("silu_ready"), sem("mods_done"), sem("gates_done"), sem("fold_done")
        tables_ready, gates_ready = sem("tables_ready"), sem("gates_ready")
        x_loaded, gate_a_loaded, gate_m_loaded = sem("x_loaded"), sem("gate_a_loaded"), sem("gate_m_loaded")
        pad_loaded, pad_ready = sem("pad_loaded"), sem("pad_ready")
        stored = sem("stored")
        stats_done_a, var_done_a, rstd_done_a, xn_done_a = sem("stats_done_a"), sem("var_done_a"), sem("rstd_done_a"), sem("xn_done_a")
        aggr_done_a = sem("aggr_done_a")
        xnT_done_a, mod_mul_a, mod_add_a = sem("xnT_done_a"), sem("mod_mul_a"), sem("mod_add_a")
        hi_done_a, lo_done_a, hi_done_m, lo_done_m = sem("hi_done_a"), sem("lo_done_a"), sem("hi_done_m"), sem("lo_done_m")
        wproj_hi, wproj_lo = sems("wproj_hi"), sems("wproj_lo")
        wqkv_hi, wqkv_lo, w1_hi, w1_lo = sems("wqkv_hi"), sems("wqkv_lo"), sems("w1_hi"), sems("w1_lo")
        qk_done, v_done = sem("qk_done"), sem("v_done")
        q_act, q_dve, k_act, k_dve = sem("q_by_act"), sem("q_by_dve"), sem("k_by_act"), sem("k_by_dve")
        v_act, v_dve = sem("v_by_act"), sem("v_by_dve")
        scores_done, masked, max_done, shifted, probs_ready = sem("scores_done"), sem("masked"), sem("max_done"), sem("shifted"), sem("probs_ready")
        probsT_done, probsT_ready, pv_done, recip_done = sem("probsT_done"), sem("probsT_ready"), sem("pv_done"), sem("recip_done")
        attn_n_ready, attn_nT_done, attnT_ready = sem("attn_n_ready"), sem("attn_nT_done"), sem("attnT_ready")
        attnT_rest = sem("attnT_rest")
        proj_done = sem("proj_done")
        res_a_ready, attn_out = sems("res_a_ready"), sems("attn_out")
        block1_ready = sem("block1_ready")
        proj_gated = sem("proj_gated")
        proj_read = [proj_gated, attn_out[1]]
        bias_a, bias_m = sem("gated_bias_a"), sem("gated_bias_m")
        stats_done_m, aggr_done_m, var_done_m, rstd_done_m, xn_done_m = sem("stats_done_m"), sem("aggr_done_m"), sem("var_done_m"), sem("rstd_done_m"), sem("xn_done_m")
        xnT_done_m, mod_mul_m, mod_add_m = sem("xnT_done_m"), sem("mod_mul_m"), sem("mod_add_m")
        up_done, gelu_done, down_done = sem("up_done"), sem("gelu_done"), sem("down_done")
        res_m_ready, mlp_out = sems("res_m_ready"), sems("mlp_out")
        down_gated = sem("down_gated")
        down_read = [down_gated, mlp_out[1]]

        x_v = a["x"].rearrange("(b t p) d -> b p t d", t=NT, p=P)
        out_v = out.rearrange("(b t p) d -> b p t d", t=NT, p=P)
        gate_v = gate_dram.rearrange("g (b t s) d -> g b s t d", t=NT, s=2)

        def col(name, k=0):
            at = COLS[name][0] + k
            return cols[:, at:at + 1]

        def row(name):
            return rows[:, ROWS.index(name), :]

        block = ctx.enter_context(nc.Block())

        @block.sync
        def _(sp):
            def load_x(b):
                sp.dma_start(attn_in(0, b)[:, :, :], x_v[b]).then_inc(x_loaded, 16)

            def load_gate(which, dst, b, loaded):
                for s in range(2):
                    src = gate_v[which, b, s]
                    sp.dma_start(dst[s * S:(s + 1) * S, :, :], src.unsqueeze(0).to_broadcast([S, NT, D])).then_inc(loaded, 8 * 2)

            def load_pad(at):
                sp.dma_start(pad_u8[:, :], a["pad"][bass.ds(at, BT)].unsqueeze(0).to_broadcast([P, BT])).then_inc(pad_loaded, 16)

            def load_stage(stages, name, loaded):
                for k in range(KT):
                    sp.dma_start(stages[k], a[name][k * P:(k + 1) * P, :]).then_inc(loaded, 16)

            wada_v = a["wada"].rearrange("(k p) n -> p k n", p=P)
            sp.dma_start(condT[:, :, :], a["condT"].rearrange("(k p) n -> p k n", p=P)).then_inc(cond_loaded, 16)
            load_x(0)
            sp.dma_start(wada[:, :, 0:2 * D], wada_v[:, :, 0:2 * D]).then_inc(wada_a_loaded, 16)
            sp.dma_start(cols[:, :], a["cols"]).then_inc(cols_loaded, 16)
            sp.dma_start(ident[:, :], a["ident"]).then_inc(ident_loaded, 16)
            load_stage(stage_wqkv[0], "wqkv0", wqkv_loaded[0])
            sp.dma_start(wada[:, :, 2 * D:], wada_v[:, :, 2 * D:]).then_inc(wada_loaded, 16)
            sp.dma_start(causal[:, :], a["causal"]).then_inc(const_loaded, 16)
            sp.dma_start(rows[:, :, :], a["rows"].unsqueeze(0).to_broadcast([P, len(ROWS), D])).then_inc(rows_loaded, 16)
            sp.dma_start(bada_gates, a["bada_gates"].unsqueeze(0).to_broadcast([NSEQ, 2, D])).then_inc(bada_loaded, 16)
            sp.dma_start(wad1, a["wad1"].rearrange("(k p) n -> p k n", p=P)).then_inc(wad1_loaded, 16)
            sp.dma_start(wad2, a["wad2"].rearrange("(k p) n -> p k n", p=P)).then_inc(wad1_loaded, 16)
            for l in range(2):
                load_stage(stage_wproj[l], f"wproj{l}", wproj_loaded[l])
                sp.dma_start(w2[l][:, :, :], a[f"w2_{l}"].rearrange("(k p) n -> p k n", p=P)).then_inc(w2_loaded[l], 16)
            sp.wait_ge(mods_done, 2)
            sp.wait_ge(gates_done, 1)
            load_stage(stage_w1[0], "w1_0", w1_loaded[0])
            load_stage(stage_wqkv[1], "wqkv1", wqkv_loaded[1])
            sp.wait_ge(gates_ready, 2)
            sp.dma_start(gate_dram.rearrange("g s d -> s g d"), gates[:, :, :]).then_inc(stored, 16)
            sp.wait_ge(stored, 16)
            load_gate(0, gate_a, 0, gate_a_loaded)
            load_gate(1, gate_m, 0, gate_m_loaded)
            sp.wait_ge(wqkv_lo[0], KT)
            sp.wait_ge(wproj_lo[1], KT)
            load_x(1)
            load_pad(0)
            sp.wait_ge(w1_lo[0], KT)
            load_stage(stage_w1[1], "w1_1", w1_loaded[1])

            def step(st):
                if st.attn:
                    _, l, b = st.attn
                    more = not (isinstance(b, int) and b == NB - 1)
                if st.mlp:
                    _, lm, bm = st.mlp
                    if lm == 1:
                        if not st.attn:
                            for t in range(NT):
                                sp.wait_ge(mlp_out[1], NT * bm + t + 1)
                                sp.dma_start(out_v[bm][:, t, :], attn_to(1, bm)[:, t, :]).then_inc(stored, 16)
                            return
                        wait(sp, mlp_out[1], NT * (bm + 1))
                        sp.dma_start(out_v[bm], attn_to(1, bm)[:, :, :]).then_inc(stored, 16)
                if st.attn and l == 0 and more:
                    wait(sp, attn_out[0], NT * (b + 1))
                    if isinstance(b, int) and b == 0:
                        load_x(2)
                    elif not (isinstance(b, int) and b == 1):
                        load_x(b + 1)
                    load_gate(0, gate_a, b + 1, gate_a_loaded)
                if st.attn and l == 1 and more:
                    wait(sp, pad_ready, b + 1)
                if st.mlp and lm == 0 and not (isinstance(bm, int) and bm == NB - 1):
                    wait(sp, down_gated, NT * (bm + 1))
                    load_gate(1, gate_m, bm + 1, gate_m_loaded)
                if st.attn and l == 1 and more:
                    load_pad((b + 1) * BT)

            schedule(sp, step)
            sp.wait_ge(stored, 16 * (NB + NT))

        @block.tensor
        def _(pe):
            seen = set()

            def first_use(sem_, value=16):
                if sem_.name not in seen:
                    seen.add(sem_.name)
                    pe.wait_ge(sem_, value)

            def norm_transposes(n, xn_done, done, banks, free):
                for part, tiles in enumerate(PARTS):
                    wait(pe, xn_done, NT * n + tiles.stop)
                    for k in range(KT):
                        if part == 0:
                            free(k)
                        for t in tiles:
                            mm = pe.transpose(banks[k][:, t * P:(t + 1) * P], xn[:, t, k * P:(k + 1) * P], ident[:, :])
                        if part == 1:
                            mm.then_inc(done, 1)

            def split_products(out_, lhs, rhs, hi_ready=None, rest_ready=None):
                terms = ((0, 0), (1, 0), (0, 1))
                passes = [(k, w, x) for k in range(KT) for w, x in terms[:2]] + [(k, *terms[2]) for k in range(KT)]
                for i, (k, w, x) in enumerate(passes):
                    if hi_ready and x == 0 and w == 0:
                        wait(pe, hi_ready[0], hi_ready[1] + k + 1)
                    if rest_ready and i == 2 * KT:
                        wait(pe, *rest_ready)
                    mm = pe.matmul(out_, lhs(k, w, x), rhs(k, w, x), start=(i == 0), stop=(i == len(passes) - 1))
                return mm

            def transposes_a(n, after_step=None):
                def free(k):
                    if after_step is not None:
                        wait(pe, masked, BS * after_step + 7 + k)
                norm_transposes(n, xn_done_a, xnT_done_a, bank_s, free)

            def transposes_m(m):
                def free(k):
                    if m_before[0] is not None:
                        lp, bp = m_before[0]
                        wait(pe, down_read[lp], NT * bp + 3 + k)
                norm_transposes(m, xn_done_m, xnT_done_m, bank_l, free)

            m_before = [None]

            def qkv(n, l, st_mlp):
                first_use(wqkv_hi[l], KT)
                first_use(wqkv_lo[l], KT)
                wait(pe, mod_mul_a, KT * (n + 1))
                for j in range(KT):
                    for c, bank in enumerate((q_bank[j], k_bank[j])):
                        at = c * D + j * P
                        split_products(bank[:, :], lambda k, w, x: wqkv[l][w][:, k, at:at + P], lambda k, w, x: xm[x][:, k, :],
                                       *(((hi_done_a, KT * n), (lo_done_a, KT * (n + 1))) if j == c == 0 else ())).then_inc(qk_done, 1)
                if st_mlp:
                    transposes_m(st_mlp[0])
                for t in range(NT):
                    if t == 2:
                        wait(pe, q_act, 6 * n + 3)
                        wait(pe, q_dve, 2 * n + 1)
                    if t == 3:
                        wait(pe, k_act, 2 * n + 2)
                    split_products(v_at[t], lambda k, w, x: xm[x][:, k, t * P:(t + 1) * P], lambda k, w, x: wqkv[l][w][:, k, 2 * D:3 * D]).then_inc(v_done, 1)

            def scores(n, l, b, s):
                if s == 0:
                    wait(pe, q_act, 6 * n + 6)
                    wait(pe, q_dve, 2 * n + 2)
                    wait(pe, k_act, 2 * n + 2)
                    wait(pe, k_dve, 2 * n + 2)
                if s >= 2:
                    wait(pe, masked, BS * n + s - 1)
                bank = bank_s[s % 2]
                for j in range(KT):
                    for u in range(2):
                        pp = 2 * j + u
                        mm = pe.matmul(bank[:, pp * P:(pp + 1) * P].rearrange("p (e k) -> p e k", e=2), qexp[:, j, s, 2 * u:2 * u + 2, :].rearrange("p a q -> p (a q)"),
                                       kpar[:, j, :, s * S:(s + 1) * S], start=True, stop=True)
                mm.then_inc(scores_done, 1)

            def probs_transposes(n, s):
                wait(pe, probs_ready, BS * n + s + 1)
                if s < 2:
                    wait(pe, v_act, 8 * n + 6 + 2 * s)
                    wait(pe, v_dve, 8 * n + 6 + 2 * s)
                else:
                    wait(pe, probsT_ready, BS * n + s - 1)
                for pp in range(PP):
                    mm = pe.transpose(bank_t[s % 2][:, pp * P:(pp + 1) * P], probs[:, s % 4, pp * P:(pp + 1) * P], ident[:, :])
                mm.then_inc(probsT_done, 1)

            def pv(n, l, s, before):
                if isinstance(n, int) and n == 0 and s == 0:
                    pe.wait_ge(gates_ready, 2)
                wait(pe, probsT_ready, BS * n + s + 1)
                wait(pe, attnT_rest, BS * n + s - 1)
                if s % 2 == 0:
                    if s >= 2:
                        wait(pe, proj_read[l], NT * before[2] + s // 2)
                    elif before[0] is not None:
                        wait(pe, proj_read[before[0]], NT * (before[1] + 1))
                for pp in range(PP):
                    mm = pe.matmul(bank_o[s % 2][:, pp * VW:(pp + 1) * VW], probsT[:, s % 2, pp * P:(pp + 1) * P], vals[:, s, pp, :], start=True, stop=True)
                mm.then_inc(pv_done, 1)

            def attn_transpose(n, s):
                wait(pe, attn_n_ready, 16 * n + 2 * s + 2)
                pe.transpose(bank_o[s % 2][:, OT0:OT0 + P], attn_n[:, s % 2, :, :, :].rearrange("p a e d -> p (a e d)"), ident[:, :]).then_inc(attn_nT_done, 1)

            def project(n, l, t):
                first_use(wproj_hi[l], KT)
                first_use(wproj_lo[l], KT)
                wait(pe, attnT_ready, BS * n + 2 * t + 2)
                wait(pe, attnT_rest, BS * n + 2 * t + 1)
                split_products(bank_o[0][:, 0:D], lambda k, w, x: attnT[x][:, k, t * P:(t + 1) * P], lambda k, w, x: wproj[l][w][:, k, :],
                               rest_ready=(attnT_rest, BS * n + 2 * t + 2)).then_inc(proj_done, 1)

            def up(m, l, c):
                first_use(w1_hi[l], KT)
                first_use(w1_lo[l], KT)
                if c == 0:
                    wait(pe, mod_mul_m, KT * (m + 1))
                if c >= 2:
                    wait(pe, gelu_done, MC * m + c - 1)
                split_products(bank_l[c % 2][:, :], lambda k, w, x: w1[l][w][:, k, c * P:(c + 1) * P], lambda k, w, x: xm[x][:, k, :],
                               *(((hi_done_m, KT * m), (lo_done_m, KT * (m + 1))) if c == 0 else ())).then_inc(up_done, 1)

            def down(m, l, b, t, first=0, end=MC, alone=False):
                first_use(w2_loaded[l])
                bank = bank_l[t % 2] if not alone else bank_s[t % 2]
                if first == 0 and t >= 2:
                    wait(pe, down_read[l], NT * b + t - 1)
                elif first == 0 and not alone:
                    wait(pe, gelu_done, MC * (m + 1))
                for c in range(first, end):
                    if alone and t == 0:
                        wait(pe, gelu_done, MC * m + c + 1)
                    mm = pe.matmul(bank[:, 0:D], hid[:, c, t * P:(t + 1) * P], w2[l][:, c, :], start=(c == 0), stop=(c == MC - 1))
                if end == MC:
                    mm.then_inc(down_done, 1)

            def mods(bank, weights, vec):
                for i, w in enumerate(weights):
                    for j in range(KT):
                        for k in range(KT):
                            o0 = (i * KT + j) * NSEQ
                            mm = pe.matmul(bank[:, o0:o0 + NSEQ], w[:, k, j * P:(j + 1) * P], vec[:, k, :], start=(k == 0), stop=(k == KT - 1))
                mm.then_inc(mods_done, 1)

            def mods_m0_and_gates():
                pe.wait_ge(wada_loaded, 16)
                pe.wait_ge(tables_ready, 1)
                mods(bank_l[0], [wada[:, :, at * D:(at + 1) * D] for at in (4, 3)], siluT)
                for g, at in enumerate((2, 5)):
                    for k in range(KT):
                        mm = pe.matmul(bank_o[0][0:NSEQ, g * D:(g + 1) * D], siluT[:, k, :], wada[:, k, at * D:(at + 1) * D], start=(k == 0), stop=(k == KT - 1))
                mm.then_inc(gates_done, 1)

            def mods_l1_and_fold():
                pe.wait_ge(wad1_loaded, 32)
                mods(bank_l[1], [w[:, :, h * D:(h + 1) * D] for w in (wad1, wad2) for h in range(2)], condT)
                first_use(wproj_hi[1], KT)
                first_use(wproj_lo[1], KT)
                pe.wait_ge(tables_ready, 2)
                for part in range(2):
                    for k in range(KT):
                        mm = pe.matmul(bank_l[0][:, 0:D], bv_wide[:, k, :], wproj[1][part][:, k, :].bitcast(F32), start=(part == k == 0), stop=(part == 1 and k == KT - 1))
                mm.then_inc(fold_done, 1)

            pe.wait_ge(silu_ready, 1)
            pe.wait_ge(wada_a_loaded, 16)
            mods(bank_l[0], [wada[:, :, at * D:(at + 1) * D] for at in (1, 0)], siluT)
            pe.wait_ge(ident_loaded, 16)
            transposes_a(0)

            def step(st):
                m_before[0] = st.before_mlp
                if st.mlp and isinstance(st.mlp[0], int) and st.mlp[0] == 0:
                    pe.wait_ge(tables_ready, 4)
                if st.attn:
                    n, l, b = st.attn
                    before = (*(st.before_attn or (None, None)), b)
                    qkv(n, l, st.mlp)
                    if isinstance(n, int) and n == 0:
                        mods_m0_and_gates()
                        pe.wait_ge(zeroed, 4)
                if st.mlp:
                    m, lm, bm = st.mlp
                if not st.attn:
                    transposes_m(m)
                    for c in range(MC):
                        up(m, lm, c)
                    for t in range(NT):
                        down(m, lm, bm, t, alone=True)
                    return
                for s in (0, 1):
                    scores(n, l, b, s)
                if isinstance(n, int) and n == 0:
                    mods_l1_and_fold()
                if st.mlp:
                    for c in range(MC // 2):
                        up(m, lm, c)
                for g in range(1, BS // 2):
                    if g == 1 or (st.mlp and g == 3):
                        scores(n, l, b, 2 * g)
                    if st.mlp and g == 1:
                        up(m, lm, 4)
                    if g == 1 or st.mlp:
                        scores(n, l, b, 2 * g + 1)
                    for s in (2 * g - 2, 2 * g - 1):
                        probs_transposes(n, s)
                    if st.mlp and g == 1:
                        up(m, lm, 5)
                    elif st.mlp:
                        down(m, lm, bm, 0 if g == 2 else 2, 0, MC if g == 2 else 4)
                    for s in (2 * g - 2, 2 * g - 1):
                        pv(n, l, s, before)
                    if g == 1 or (g == 2 and not st.mlp):
                        scores(n, l, b, 2 * g + 2)
                    if st.mlp and g == 1:
                        up(m, lm, 6)
                    elif st.mlp and g == 2:
                        down(m, lm, bm, 1, 0, 4)
                    elif st.mlp:
                        down(m, lm, bm, 2, 4, 6)
                    for s in (2 * g - 2, 2 * g - 1):
                        attn_transpose(n, s)
                    if st.mlp and g == 1:
                        up(m, lm, 7)
                    elif st.mlp and g == 2:
                        down(m, lm, bm, 1, 4, MC)
                    elif st.mlp:
                        down(m, lm, bm, 2, 6, MC)
                    if g < 3 and not st.mlp:
                        scores(n, l, b, 2 * g + 3)
                    project(n, l, g - 1)
                for s in (6, 7):
                    probs_transposes(n, s)
                if st.nxt and not st.late:
                    transposes_a(st.nxt[0], after_step=n)
                if st.mlp:
                    down(m, lm, bm, 3, 0, 4)
                for s in (6, 7):
                    pv(n, l, s, before)
                if st.mlp:
                    down(m, lm, bm, 3, 4, 6)
                for s in (6, 7):
                    attn_transpose(n, s)
                if st.late:
                    down(m, lm, bm, 3, 6, 7)
                    project(n, l, 3)
                    down(m, lm, bm, 3, 7, MC)
                else:
                    if st.mlp:
                        down(m, lm, bm, 3, 6, MC)
                    project(n, l, 3)
                if st.nxt and st.late:
                    transposes_a(st.nxt[0], after_step=n)

            bv_wide = cols[:, COLS["bv"][0]:COLS["bv"][0] + KT].unsqueeze(2).to_broadcast([P, KT, P])
            pe.wait_ge(cols_loaded, 16)
            schedule(pe, step)

        @block.vector
        def _(dve):
            def tile_stats(n, x, t, arrived, st_, done, aggr):
                wait(dve, *arrived)
                wait(dve, aggr, NT * n)
                dve.bn_stats(st_[:, t, :], x[:, t, :]).then_inc(done, 1)

            def variances(n, part, st_, mv, ve, done, aggr, var, read):
                tiles = PARTS[part]
                wait(dve, done, NT * n + tiles.stop)
                wait(dve, read, NT * n)
                dve.memset(carrier[:, :], 0.0)
                for t in tiles:
                    dve.bn_aggr(mv[:, t, :], st_[:, t, :]).then_inc(aggr, 1)
                wait(dve, aggr, NT * n + tiles.stop)
                dve.tensor_scalar(ve[:, tiles.start:tiles.stop], mv[:, tiles.start:tiles.stop, 1], EPS, None, ALU.add).then_inc(var, 1)

            def normalise(n, part, x, mv, rstd, rstd_done, done):
                wait(dve, rstd_done, 2 * n + part + 1)
                for t in PARTS[part]:
                    dve.tensor_scalar(xn[:, t, :], x[:, t, :], mv[:, t, 0:1], rstd[:, t:t + 1], ALU.subtract, ALU.mult).then_inc(done, 1)

            def modulate(n, l, b, norm, banks, xnT_done, mul, add, last=None, soon=False):
                if last:
                    wait(dve, *last)
                def times(k):
                    wait(dve, xnT_done, KT * n + k + 1)
                    src = banks[k][:, :].rearrange("p (s q) -> p s q", q=S)
                    tmp = tmp_mod[:, k, :].rearrange("p (s q) -> p s q", q=S)
                    factor = mod_mul[:, l, norm, k, bass.ds(BS * b, BS)].unsqueeze(2).to_broadcast([P, BS, S])
                    dve.tensor_tensor(tmp, src, factor, ALU.mult).then_inc(mul, 1)

                def plus(k):
                    wait(dve, mul, KT * n + k + 1)
                    tmp = tmp_mod[:, k, :].rearrange("p (s q) -> p s q", q=S)
                    term = mod_add[:, l, norm, k, bass.ds(BS * b, BS)].unsqueeze(2).to_broadcast([P, BS, S])
                    dve.tensor_tensor(tmp, tmp, term, ALU.add).then_inc(add, 1)

                for k in range(KT):
                    times(k)
                    if soon:
                        plus(k)
                if not soon:
                    for k in range(KT):
                        plus(k)

            def rest(n, hi, lo, tiles=range(KT)):
                for k in tiles:
                    wait(dve, hi, KT * n + k + 1)
                    dve.tensor_tensor(xm[1][:, k, :], tmp_mod[:, k, :], xm[0][:, k, :].bitcast(F32), ALU.subtract).then_inc(lo, 1)

            def tile_stats_a(n, l, b, t):
                arrived = (x_loaded, 16 * (b + 1)) if l == 0 else (mlp_out[0], NT * b + t + 1)
                tile_stats(n, attn_in(l, b), t, arrived, stats_a_buf, stats_done_a, aggr_done_a)

            def variances_a(n, part):
                variances(n, part, stats_a_buf, mv_a, ve_a, stats_done_a, aggr_done_a, var_done_a, xn_done_a)

            def stats_a(n, l, b):
                for t in range(NT):
                    tile_stats_a(n, l, b, t)
                for part in range(2):
                    variances_a(n, part)

            def normalise_a(n, l, b, m=-1, parts=(0, 1)):
                wait(dve, xnT_done_m, KT * (m + 1))
                for part in parts:
                    normalise(n, part, attn_in(l, b), mv_a, rstd_a, rstd_done_a, xn_done_a)

            def modulate_a(n, l, b, m=None, soon=False):
                modulate(n, l, b, 0, bank_s, xnT_done_a, mod_mul_a, mod_add_a, None if m is None else (lo_done_m, KT * (m + 1)), soon)

            def tile_stats_m(m, l, b, t):
                tile_stats(m, attn_to(l, b), t, (attn_out[l], NT * b + t + 1), stats_m, stats_done_m, aggr_done_m)

            def variances_m(m, part):
                variances(m, part, stats_m, mv_m, ve_m, stats_done_m, aggr_done_m, var_done_m, xn_done_m)

            def normalise_mlp(m, l, b, n):
                wait(dve, xnT_done_a, KT * (n + 1))
                for part in range(2):
                    normalise(m, part, attn_to(l, b), mv_m, rstd_m, rstd_done_m, xn_done_m)

            def queries(n, l, j):
                wait(dve, qk_done, 4 * n + 2 * j + 1)
                wait(dve, scores_done, BS * n)
                for pr in (3,):
                    r = slice(32 * pr, 32 * pr + 32)
                    dst, src = qexp[r, j, :, pr, :], q_bank[j][r, :].rearrange("p (s q) -> p s q", q=S)
                    if l == 0:
                        i = dve.tensor_copy(dst, src)
                    else:
                        i = dve.tensor_scalar(dst, src, cols[r, COLS["bq"][0] + j:COLS["bq"][0] + j + 1], None, ALU.add)
                    i.then_inc(q_dve, 1)

            def keys(n, l):
                wait(dve, qk_done, 4 * n + 4)
                for e, name in enumerate(("even", "odd")):
                    if l == 0:
                        i = dve.tensor_scalar(kpar[:, 1, e, :], k_bank[1][:, :], col(name), None, ALU.mult)
                    else:
                        i = dve.tensor_scalar(kpar[:, 1, e, :], k_bank[1][:, :], col("bk", 1), col(name), ALU.add, ALU.mult)
                    i.then_inc(k_dve, 1)

            def values(n, t):
                wait(dve, v_done, NT * n + max(t + 1, 2))
                wait(dve, pv_done, BS * n)
                src = v_at[t][S:2 * S, :].rearrange("p (a b e d) -> p a b e d", a=PP, b=2, e=2)
                for e in range(2):
                    dst = vals[e * S:(e + 1) * S, 2 * t + 1, :, 0:4 * HD].rearrange("p a (b e d) -> p a b e d", b=2, e=2)
                    dve.tensor_copy(dst[:, :, :, e, :], src[:, :, :, e, :]).then_inc(v_dve, 1)

            def pad_mask(n, b):
                wait(dve, pad_loaded, 16 * (b + 1))
                wait(dve, masked, BS * n)
                dve.tensor_scalar(pad_bf[:, :], pad_u8[:, :], MASKED, None, ALU.mult).then_inc(pad_ready, 1)

            def shift(n, l, b, s):
                at = probs[:, s % 4, :].rearrange("p (g k) -> p g k", k=S)
                mask = causal[:, :] if l == 0 else pad_bf[:, s * S:(s + 1) * S]
                if l == 1 and s == 0:
                    wait(dve, pad_ready, b + 1)
                wait(dve, scores_done, BS * n + s + 1)
                wait(dve, probsT_done, BS * n + s - 3)
                dve.tensor_tensor(at, bank_s[s % 2][:, :].rearrange("p (g k) -> p g k", k=S), mask.unsqueeze(1).to_broadcast([P, H // 2, S]), ALU.add).then_inc(masked, 1)
                wait(dve, masked, BS * n + s + 1)
                dve.tensor_reduce(row_max[:, s % 2, :], at, AX.X, ALU.max).then_inc(max_done, 1)
                wait(dve, max_done, BS * n + s + 1)
                dve.tensor_tensor(at, at, row_max[:, s % 2, :].unsqueeze(2).to_broadcast([P, H // 2, S]), ALU.subtract).then_inc(shifted, 1)

            def divide(n, s):
                bank = bank_o[s % 2][:, 0:PP * VW].rearrange("p (a w) -> p a w", a=PP)
                wait(dve, pv_done, BS * n + s + 1)
                dve.reciprocal(recip[:, s % 2, :, :], bank[:, :, 4 * HD:4 * HD + 2]).then_inc(recip_done, 1)
                wait(dve, recip_done, BS * n + s + 1)
                wait(dve, attn_nT_done, BS * n + s - 1)
                for b in range(2):
                    r = slice(b * S, (b + 1) * S)
                    src = bank[r, :, b * 2 * HD:(b + 1) * 2 * HD].rearrange("p a (e d) -> p a e d", e=2)
                    dve.tensor_tensor(attn_n[r, s % 2, :, :, :], src, recip[r, s % 2, :, :].unsqueeze(3).to_broadcast([S, PP, 2, HD]), ALU.mult).then_inc(attn_n_ready, 1)

            def rest_attnT(n, s):
                wait(dve, attnT_ready, BS * n + s + 1)
                if s == 0:
                    wait(dve, proj_done, NT * n)
                at = attnT[0][:, :, s * S:(s + 1) * S]
                dve.tensor_tensor(attnT[1][:, :, s * S:(s + 1) * S], bank_o[s % 2][:, OT0:OT0 + P].rearrange("p (k q) -> p k q", k=KT), at.bitcast(F32), ALU.subtract).then_inc(attnT_rest, 1)

            def add_projection(n, l, b, t):
                wait(dve, proj_done, NT * n + t + 1)
                if l == 0:
                    wait(dve, gate_a_loaded, 32 * (b + 1))
                    dve.tensor_tensor(gated_a[:, t % 2, :], bank_o[0][:, 0:D], gate_a[:, t, :], ALU.mult).then_inc(proj_gated, 1)
                    wait(dve, proj_gated, NT * b + t + 1)
                    src = gated_a[:, t % 2, :]
                else:
                    src = bank_o[0][:, 0:D]
                wait(dve, res_a_ready[l], NT * b + t + 1)
                if isinstance(n, int) and n == 1:
                    dve.tensor_tensor(src, src, attn_in(l, b)[:, t, :], ALU.add).then_inc(block1_ready, 1)
                    return
                if l == 0:
                    wait(dve, mlp_out[0], NT * b)
                elif isinstance(b, int) and b == NB - 1:
                    dve.wait_ge(mlp_out[0], NT * NB)
                else:
                    wait(dve, stored, 16 * (b + 1))
                dve.tensor_tensor(attn_to(l, b)[:, t, :], src, attn_in(l, b)[:, t, :], ALU.add).then_inc(attn_out[l], 1)

            def take_place(t):
                dve.wait_ge(block1_ready, t + 1)
                dve.wait_ge(mlp_out[0], t + 1)
                dve.tensor_copy(x_attn[0][:, t, :], gated_a[:, t % 2, :]).then_inc(attn_out[0], 1)

            def add_down(m, l, b, t, banks=bank_l):
                wait(dve, down_done, NT * m + t + 1)
                if l == 0:
                    wait(dve, gate_m_loaded, 32 * (b + 1))
                    dve.tensor_tensor(gated_m[:, t % 2, :], banks[t % 2][:, 0:D], gate_m[:, t, :], ALU.mult).then_inc(down_gated, 1)
                    wait(dve, down_gated, NT * b + t + 1)
                    src = gated_m[:, t % 2, :]
                    if isinstance(b, int) and b == 0:
                        dve.wait_ge(block1_ready, t + 1)
                    else:
                        wait(dve, attn_out[1], NT * (b - 1) + t + 1)
                else:
                    src = banks[t % 2][:, 0:D]
                wait(dve, res_m_ready[l], NT * b + t + 1)
                dve.tensor_tensor(mlp_to(l, b)[:, t, :], src, attn_to(l, b)[:, t, :], ALU.add).then_inc(mlp_out[l], 1)

            dve.wait_ge(setup_exp, 1)
            dve.tensor_scalar(siluT[:, :, :], siluT[:, :, :], 1.0, None, ALU.add).then_inc(setup_dve, 1)
            dve.wait_ge(setup_dve, 1)
            dve.reciprocal(siluT[:, :, :], siluT[:, :, :]).then_inc(setup_dve, 1)
            dve.wait_ge(setup_dve, 2)
            dve.tensor_tensor(siluT[:, :, :], siluT[:, :, :], condT[:, :, :], ALU.mult).then_inc(silu_ready, 1)
            stats_a(0, 0, 0)
            normalise_a(0, 0, 0)
            dve.wait_ge(cols_loaded, 16)
            for i, name in enumerate(("bada_sc_a", "bada_sc_m", "sc1_1", "sc2_1")):
                at = COLS[name][0]
                dve.tensor_scalar(col1[:, 2 * i:2 * i + 2], cols[:, at:at + 2], 1.0, None, ALU.add).then_inc(setup_dve, 1)

            def table_l0(norm, g, be, sh):
                earlier = 6 + 4 * norm
                for k in range(KT):
                    sc_ps = bank_l[0][:, k * NSEQ:(k + 1) * NSEQ]
                    one = col1[:, 2 * norm + k:2 * norm + k + 1]
                    dve.tensor_scalar(mod_mul[:, 0, norm, k, :], sc_ps, one, col(g, k), ALU.add, ALU.mult).then_inc(setup_dve, 1)
                    dve.tensor_scalar(table_tmp[:, k, :], sc_ps, one, col(be, k), ALU.add, ALU.mult).then_inc(setup_dve, 1)
                for k in range(KT):
                    sh_ps = bank_l[0][:, (KT + k) * NSEQ:(KT + k + 1) * NSEQ]
                    dve.wait_ge(setup_dve, earlier + 2 * k + 2)
                    i = dve.scalar_tensor_tensor(out=mod_add[:, 0, norm, k, :], in0=sh_ps, scalar=col(sh, k), in1=table_tmp[:, k, :], op0=ALU.add, op1=ALU.add)
                i.then_inc(tables_ready, 1)

            def table_m0_and_gates():
                dve.wait_ge(mods_done, 2)
                dve.wait_ge(tables_ready, 1)
                table_l0(1, "g2", "be2", "bada_sh_m")
                dve.wait_ge(gates_done, 1)
                dve.wait_ge(bada_loaded, 16)
                for g in range(2):
                    dve.tensor_tensor(gates[:, g, :], bank_o[0][0:NSEQ, g * D:(g + 1) * D], bada_gates[:, g, :], ALU.add).then_inc(gates_ready, 1)

            def tables_l1_and_fold():
                dve.wait_ge(mods_done, 3)
                for norm, sh in enumerate(("sh1_1", "sh2_1")):
                    for k in range(KT):
                        sc_ps = bank_l[1][:, (2 * norm * KT + k) * NSEQ:(2 * norm * KT + k + 1) * NSEQ]
                        sh_ps = bank_l[1][:, ((2 * norm + 1) * KT + k) * NSEQ:((2 * norm + 1) * KT + k + 1) * NSEQ]
                        dve.tensor_scalar(mod_mul[:, 1, norm, k, :], sc_ps, col1[:, 4 + 2 * norm + k:5 + 2 * norm + k], None, ALU.add)
                        i = dve.tensor_scalar(mod_add[:, 1, norm, k, :], sh_ps, col(sh, k), None, ALU.add)
                i.then_inc(tables_ready, 1)
                dve.wait_ge(fold_done, 1)
                dve.wait_ge(rows_loaded, 16)
                dve.tensor_tensor(row("bproj_1"), bank_l[0][:, 0:D], row("bproj_1"), ALU.add).then_inc(tables_ready, 1)

            dve.wait_ge(setup_dve, 6)
            dve.wait_ge(mods_done, 1)
            table_l0(0, "g1", "be1", "bada_sh_a")
            dve.wait_ge(tables_ready, 1)
            modulate_a(0, 0, 0, soon=True)
            dve.wait_ge(const_loaded, 16)
            rest(0, hi_done_a, lo_done_a)
            dve.wait_ge(zeroed, 4)

            def step(st):
                m = None
                if st.mlp:
                    m, lm, bm = st.mlp
                if not st.attn:
                    normalise_mlp(m, lm, bm, m)
                    modulate(m, lm, bm, 1, bank_l, xnT_done_m, mod_mul_m, mod_add_m, soon=True)
                    rest(m, hi_done_m, lo_done_m)
                    for t in range(NT):
                        add_down(m, lm, bm, t, bank_s)
                    return
                n, l, b = st.attn
                queries(n, l, 0)
                if st.mlp:
                    normalise_mlp(m, lm, bm, n)
                queries(n, l, 1)
                keys(n, l)
                if isinstance(n, int) and n == 1:
                    dve.wait_ge(tables_ready, 4)
                if st.mlp:
                    modulate(m, lm, bm, 1, bank_l, xnT_done_m, mod_mul_m, mod_add_m, (lo_done_a, KT * (n + 1)))
                for t in range(NT):
                    if st.mlp and t == 1:
                        rest(m, hi_done_m, lo_done_m)
                    values(n, t)
                if isinstance(n, int) and n == 0:
                    table_m0_and_gates()
                shift(n, l, b, 0)
                shift(n, l, b, 1)
                if isinstance(n, int) and n == 0:
                    tables_l1_and_fold()

                both_l0 = st.mlp and lm == l == 0

                def finish_mlp_tile(t):
                    add_down(m, lm, bm, t)
                    if st.late:
                        tile_stats_a(*st.nxt, t)
                        if t == NT - 1:
                            variances_a(st.nxt[0], 1)
                    if both_l0:
                        take_place(t)
                        tile_stats_m(n, l, b, t)

                def finish_tiles(t):
                    for s in (2 * t, 2 * t + 1):
                        rest_attnT(n, s)
                    if t == 2 and st.nxt and not st.late:
                        normalise_a(*st.nxt, m if st.mlp else -1, (1,))
                    if t == 2 and st.nxt and st.nxt[1] == 1:
                        pad_mask(st.nxt[0], st.nxt[2])
                    if t == 3 and st.nxt and not st.late:
                        rest(st.nxt[0], hi_done_a, lo_done_a, (1,))
                    if st.mlp and t == 1:
                        finish_mlp_tile(0)
                    if t == 3 and st.late:
                        variances_a(st.nxt[0], 0)
                    if t == 3:
                        variances_m(n, 0)
                    add_projection(n, l, b, t)
                    if not both_l0:
                        tile_stats_m(n, l, b, t)
                    if t == 3 and st.late:
                        normalise_a(*st.nxt, m, (0,))
                    elif t == 3:
                        variances_m(n, 1)
                    if st.mlp and t > 0:
                        finish_mlp_tile(t)

                for g in range(1, BS // 2):
                    if g == 1 or (st.mlp and g == 3):
                        shift(n, l, b, 2 * g)
                    if g == 1 or st.mlp:
                        shift(n, l, b, 2 * g + 1)
                    divide(n, 2 * g - 2)
                    divide(n, 2 * g - 1)
                    if g == 1 or (g == 2 and not st.mlp):
                        shift(n, l, b, 2 * g + 2)
                    if g < 3 and not st.mlp:
                        finish_tiles(g - 1)
                        shift(n, l, b, 2 * g + 3)
                    if g == 2 and st.nxt and not st.late:
                        stats_a(*st.nxt)
                    if g == 3 and st.nxt and not st.late:
                        normalise_a(*st.nxt, m if st.mlp else -1, (0,))
                    if g == 3 or st.mlp:
                        finish_tiles(g - 1)
                if st.nxt and not st.late:
                    modulate_a(*st.nxt, m)
                divide(n, 6)
                divide(n, 7)
                if st.nxt and not st.late:
                    rest(st.nxt[0], hi_done_a, lo_done_a, (0,))
                finish_tiles(3)
                if st.late:
                    variances_m(n, 1)
                    normalise_a(*st.nxt, m, (1,))
                    modulate_a(*st.nxt, m, soon=True)
                    rest(st.nxt[0], hi_done_a, lo_done_a)

            schedule(dve, step)

        @block.scalar
        def _(act):
            def queries(n, l, j):
                wait(act, qk_done, 4 * n + 2 * j + 1)
                wait(act, scores_done, BS * n)
                for pr in (0, 1, 2):
                    r = slice(32 * pr, 32 * pr + 32)
                    bias = 0.0 if l == 0 else cols[r, COLS["bq"][0] + j:COLS["bq"][0] + j + 1]
                    act.activation(qexp[r, j, :, pr, :], q_bank[j][r, :].rearrange("p (s q) -> p s q", q=S), ACT.Identity, bias=bias).then_inc(q_act, 1)

            def keys(n, l):
                wait(act, qk_done, 4 * n + 2)
                for e, name in enumerate(("even", "odd")):
                    bias = 0.0 if l == 0 else bk_par[:, e:e + 1]
                    act.activation(kpar[:, 0, e, :], k_bank[0][:, :], ACT.Identity, bias=bias, scale=col(name)).then_inc(k_act, 1)

            def values(n, t):
                wait(act, v_done, NT * n + max(t + 1, 2))
                wait(act, pv_done, BS * n)
                src = v_at[t][0:S, :].rearrange("p (a b e d) -> p a b e d", a=PP, b=2, e=2)
                for e in range(2):
                    dst = vals[e * S:(e + 1) * S, 2 * t, :, 0:4 * HD].rearrange("p a (b e d) -> p a b e d", b=2, e=2)
                    act.activation(dst[:, :, :, e, :], src[:, :, :, e, :], ACT.Copy).then_inc(v_act, 1)

            def exps(n, s):
                wait(act, shifted, BS * n + s + 1)
                act.activation(probs[:, s % 4, :], probs[:, s % 4, :], ACT.Exp, scale=SCALE).then_inc(probs_ready, 1)

            def read_probsT(n, s):
                wait(act, probsT_done, BS * n + s + 1)
                wait(act, pv_done, BS * n + s - 1)
                act.activation(probsT[:, s % 2, :], bank_t[s % 2][:, :], ACT.Copy).then_inc(probsT_ready, 1)

            def read_attnT(n, s):
                wait(act, attn_nT_done, BS * n + s + 1)
                if s == 0:
                    wait(act, proj_done, NT * n)
                act.activation(attnT[0][:, :, s * S:(s + 1) * S], bank_o[s % 2][:, OT0:OT0 + P].rearrange("p (k q) -> p k q", k=KT), ACT.Copy).then_inc(attnT_ready, 1)

            def load_gelu():
                act.wait_ge(pool_const, 1)
                act.activation(gelu_carrier[:, :], half_neg[:, 0:1], ACT.Gelu)

            def gelu(m, l, c):
                wait(act, up_done, MC * m + c + 1)
                if c == 0 and isinstance(m, int) and m == 0:
                    act.wait_ge(w1_lo[0], KT)
                    act.wait_ge(wqkv_lo[1], KT)
                    act.wait_ge(w1_lo[1], KT)
                elif c == 0:
                    wait(act, down_done, NT * m)
                act.activation(hid[:, c, :], bank_l[c % 2][:, :], ACT.Gelu, bias=col(f"b1_{l}", c)).then_inc(gelu_done, 1)

            def modulated_hi(n, add, hi, read=None):
                if read:
                    wait(act, *read)
                for k in range(KT):
                    wait(act, add, KT * n + k + 1)
                    act.activation(xm[0][:, k, :], tmp_mod[:, k, :], ACT.Copy).then_inc(hi, 1)

            def weights_hi(stages, w, loaded, hi):
                act.wait_ge(loaded, 16 * KT)
                for k in range(KT):
                    act.activation(w[0][:, k, :], stages[k], ACT.Copy).then_inc(hi, 1)

            act.wait_ge(cond_loaded, 16)
            act.activation(siluT[:, :, :], condT[:, :, :], ACT.Exp, scale=-1.0).then_inc(setup_exp, 1)
            act.wait_ge(cols_loaded, 16)
            for e, name in enumerate(("even", "odd")):
                act.activation(bk_par[:, e:e + 1], col("bk"), ACT.Identity, scale=col(name)).then_inc(bk_ready, 1)
            weights_hi(stage_wqkv[0], wqkv[0], wqkv_loaded[0], wqkv_hi[0])
            modulated_hi(0, mod_add_a, hi_done_a)
            act.wait_ge(bk_ready, 2)
            act.wait_ge(zeroed, 4)

            def step(st):
                if st.mlp:
                    m, lm, bm = st.mlp
                if not st.attn:
                    load_gelu()
                    modulated_hi(m, mod_add_m, hi_done_m)
                    for c in range(MC):
                        gelu(m, lm, c)
                    return
                n, l, b = st.attn
                queries(n, l, 0)
                keys(n, l)
                queries(n, l, 1)
                for t in range(NT):
                    values(n, t)
                if isinstance(n, int) and n == 0:
                    for i in (1, 0):
                        weights_hi(stage_wproj[i], wproj[i], wproj_loaded[i], wproj_hi[i])
                if st.mlp:
                    modulated_hi(m, mod_add_m, hi_done_m, (v_done, NT * (n + 1)))
                    load_gelu()
                    for c in range(MC // 2):
                        gelu(m, lm, c)
                exps(n, 0)
                exps(n, 1)
                for g in range(1, BS // 2):
                    read_probsT(n, 2 * g - 2)
                    read_probsT(n, 2 * g - 1)
                    exps(n, 2 * g)
                    exps(n, 2 * g + 1)
                    if st.mlp and g == 1:
                        for c in (4, 5, 6):
                            gelu(m, lm, c)
                    read_attnT(n, 2 * g - 2)
                    read_attnT(n, 2 * g - 1)
                    if st.mlp and g == 1:
                        gelu(m, lm, 7)
                    if isinstance(n, int) and n == 0 and g == 1:
                        weights_hi(stage_w1[0], w1[0], w1_loaded[0], w1_hi[0])
                    if isinstance(n, int) and n == 0 and g == 2:
                        weights_hi(stage_wqkv[1], wqkv[1], wqkv_loaded[1], wqkv_hi[1])
                read_probsT(n, 6)
                read_probsT(n, 7)
                if st.nxt and not st.late:
                    modulated_hi(st.nxt[0], mod_add_a, hi_done_a)
                read_attnT(n, 6)
                read_attnT(n, 7)
                if isinstance(n, int) and n == 0:
                    weights_hi(stage_w1[1], w1[1], w1_loaded[1], w1_hi[1])
                if st.late:
                    modulated_hi(st.nxt[0], mod_add_a, hi_done_a)

            schedule(act, step)

        @block.gpsimd
        def _(pool):
            def rstd(n, part, ve, out_, var, xn_done, done):
                at = slice(PARTS[part].start, PARTS[part].stop)
                wait(pool, var, 2 * n + part + 1)
                wait(pool, xn_done, NT * n)
                pool.tensor_tensor(out_[:, at], ve[:, at], half_neg[:, at], ALU.pow).then_inc(done, 1)

            def rstd_attn(n, part):
                rstd(n, part, ve_a, rstd_a, var_done_a, xn_done_a, rstd_done_a)

            def rstd_mlp(m, part):
                rstd(m, part, ve_m, rstd_m, var_done_m, xn_done_m, rstd_done_m)

            def residual(l, b, kind, xn_done, count):
                x, gate, loaded, ready, gated, bias = ((attn_in(l, b), gate_a, gate_a_loaded, res_a_ready, bias_a, row(f"bproj_{l}")) if kind == "a" else
                                                       (attn_to(l, b), gate_m, gate_m_loaded, res_m_ready, bias_m, row(f"b2_{l}")))
                if l == 0:
                    wait(pool, loaded, 32 * (b + 1))
                wait(pool, xn_done, count)
                for t in range(NT):
                    if l == 0:
                        pool.tensor_tensor(gate_bias[:, t % 2, :], gate[:, t, :], bias, ALU.mult).then_inc(gated, 1)
                        wait(pool, gated, NT * b + t + 1)
                    pool.tensor_tensor(x[:, t, :], x[:, t, :], gate_bias[:, t % 2, :] if l == 0 else bias, ALU.add).then_inc(ready[l], 1)

            def weights_rest(stages, w, hi, lo):
                for k in range(KT):
                    pool.wait_ge(hi, k + 1)
                    pool.tensor_tensor(w[1][:, k, :], stages[k], w[0][:, k, :].bitcast(F32), ALU.subtract).then_inc(lo, 1)

            pool.memset(half_neg[:, :], -0.5).then_inc(pool_const, 1)
            pool.memset(vals[:, :, :, :], 0.0).then_inc(zeroed, 1)
            pool.wait_ge(pool_const, 1)
            for part in range(2):
                rstd_attn(0, part)
            weights_rest(stage_wqkv[0], wqkv[0], wqkv_hi[0], wqkv_lo[0])
            pool.memset(qexp[:, :, :, :, :], 0.0).then_inc(zeroed, 1)
            pool.wait_ge(zeroed, 2)
            for e in range(2):
                pool.memset(vals[e * S:(e + 1) * S, :, :, 4 * HD + e:4 * HD + e + 1], 1.0).then_inc(zeroed, 1)
            pool.wait_ge(zeroed, 4)
            for l in (1, 0):
                weights_rest(stage_wproj[l], wproj[l], wproj_hi[l], wproj_lo[l])
            pool.wait_ge(rows_loaded, 16)

            def step(st):
                if st.mlp:
                    m, lm, bm = st.mlp
                if st.attn:
                    if isinstance(st.attn[0], int) and st.attn[0] == 2:
                        pool.wait_ge(tables_ready, 4)
                    residual(st.attn[1], st.attn[2], "a", xn_done_a, NT * (st.attn[0] + 1))
                if st.mlp:
                    residual(lm, bm, "m", xn_done_m, NT * (m + 1))
                if st.nxt and not st.late:
                    for part in range(2):
                        rstd_attn(st.nxt[0], part)
                if st.attn and isinstance(st.attn[0], int) and st.attn[0] == 0:
                    weights_rest(stage_w1[0], w1[0], w1_hi[0], w1_lo[0])
                    weights_rest(stage_wqkv[1], wqkv[1], wqkv_hi[1], wqkv_lo[1])
                    weights_rest(stage_w1[1], w1[1], w1_hi[1], w1_lo[1])
                if st.attn:
                    for part in range(2):
                        if st.late:
                            rstd_attn(st.nxt[0], part)
                        rstd_mlp(st.attn[0], part)

            schedule(pool, step)


def layer_columns(v):
    return np.asarray(v).reshape(-1, P).T


def by_pair_parity(w):
    w = np.asarray(w)
    return w.reshape(PP, 2, 2 * HD, -1).transpose(1, 0, 2, 3).reshape(w.shape)


def kernel(**inputs):
    import concourse.bacc as bacc
    from concourse.bass_utils import run_bass_kernel_spmd

    v = {k: np.asarray(x) for k, x in inputs.items()}
    L0 = {k[8:]: x for k, x in v.items() if k.startswith("L0_cond_")}
    L1 = {k[8:]: x for k, x in v.items() if k.startswith("L1_cond_")}
    f32 = np.float32
    even = (np.arange(P) // HD % 2 == 0).astype(f32)
    bada, ad1, ad2 = L0["bada"].reshape(6, D), L1["b_adaln1"].reshape(2, D), L1["b_adaln2"].reshape(2, D)
    vectors = {
        "g1": L0["g1"], "be1": L0["be1"], "g2": L0["g2"], "be2": L0["be2"],
        "bada_sc_a": bada[1], "bada_sh_a": bada[0], "bada_sc_m": bada[4], "bada_sh_m": bada[3], "b1_0": L0["b1"],
        "sc1_1": ad1[0], "sh1_1": ad1[1], "sc2_1": ad2[0], "sh2_1": ad2[1],
        "bq": L1["bq"], "bk": L1["bk"], "bv": by_pair_parity(L1["bv"]), "b1_1": L1["b1"],
        "even": even, "odd": np.where(even > 0, f32(0), f32(1)),
    }
    bf16 = mybir.dt.np(BF16)
    q, k = np.arange(P)[:, None] % S, np.arange(S)[None, :]
    arrays = {
        "x": v["x"].reshape(NSEQ * S, D),
        "pad": v["mask_BxS_bf0"].reshape(-1),
        "condT": v["cond_1024"].T,
        "cols": np.concatenate([layer_columns(vectors[name]) for name in COLS], axis=1),
        "rows": np.stack([L0["bproj"], L1["bo"], L0["b2"], L1["b2"]]),
        "bada_gates": np.stack([bada[2], bada[5]]),
        "ident": np.eye(P, dtype=f32),
        "causal": np.where(k <= q, 0.0, MASKED).astype(bf16),
        "wada": L0["Wada"],
        "wad1": L1["w_adaln1"].T, "wad2": L1["w_adaln2"].T,
        "wqkv0": L0["Wqkv"], "wqkv1": np.concatenate([L1["wq"].T, L1["wk"].T, L1["wv"].T], axis=1),
        "wproj0": by_pair_parity(L0["Wproj"]), "wproj1": by_pair_parity(L1["wo"].T),
        "w1_0": L0["W1"], "w1_1": L1["w1"].T,
        "w2_0": L0["W2"], "w2_1": L1["w2"].T,
    }
    arrays = {k_: np.ascontiguousarray(x) for k_, x in arrays.items()}
    nc = bacc.Bacc("TRN2", target_bir_lowering=False, num_devices=1)
    aps = {k_: nc.dram_tensor(f"in_{k_}", x.shape, mybir.dt.from_np(x.dtype), kind="ExternalInput").ap() for k_, x in arrays.items()}
    out = nc.dram_tensor("out", (NSEQ * S, D), F32, kind="ExternalOutput").ap()
    build(nc, aps, out)
    r = run_bass_kernel_spmd(nc, [{f"in_{k_}": x for k_, x in arrays.items()}], core_ids=[0])
    return r.results[0]["out"].reshape(NSEQ, S, D)
```
